# Optimizing a Trainium2 kernel written in Bass

```python
import numpy as np
import jax
import jax.numpy as jnp

def _softmax(x, axis=-1):
    return jax.nn.softmax(x, axis=axis)

def _gelu(x):
    return jax.nn.gelu(x, approximate=True)

def _silu(x):
    return jax.nn.silu(x)

def _sigmoid(x):
    return jax.nn.sigmoid(x)

def _layernorm(x, axis=-1, eps=1e-05):
    m = jnp.mean(x, axis=axis, keepdims=True)
    v = jnp.var(x, axis=axis, keepdims=True)
    return (x - m) / jnp.sqrt(v + eps)

def _scatter_add(tgt, idx, src, axis=0):
    return tgt.at[idx].add(src)

def _segment_sum(src, seg, n):
    return jax.ops.segment_sum(src, seg, n)
kernel_name = 'mk_vit_tower_d1_tok_img256_r4_4eb591'

def setup_inputs(seed: int=0):
    np.random.seed(seed)
    _w = jnp.asarray

    def _rec_inputs():
        import jax
        import jax.numpy as jnp
        _rk = jax.random.key(seed)
        x = -0.000596345 + 1.00056 * jax.random.normal(jax.random.fold_in(_rk, 1), (128, 64, 64, 3), jnp.float32)
        return x
    x = _rec_inputs()

    def _L0_tok_setup():
        import jax, jax.numpy as jnp
        import numpy as np
        B, H, W = (16, 64, 64)
        WIDTH, LAYERS, M1, M2 = (32, 4, 12, 12)
        EPS = 1e-05

        def layer_norm(x, g, b):
            mu = jnp.mean(x, axis=-1, keepdims=True)
            var = jnp.mean((x - mu) ** 2, axis=-1, keepdims=True)
            return (x - mu) * jax.lax.rsqrt(var + EPS) * g + b

        def gelu(x):
            return jax.nn.gelu(x, approximate=False)

        def spectral_conv(x, w1, w2):
            b, c, h, w = x.shape
            x_ft = jnp.fft.rfft2(x)
            out_ft = jnp.zeros((b, w1.shape[1], h, w // 2 + 1), dtype=x_ft.dtype)
            out_ft = out_ft.at[:, :, :M1, :M2].set(jnp.einsum('bixy,ioxy->boxy', x_ft[:, :, :M1, :M2], w1))
            out_ft = out_ft.at[:, :, -M1:, :M2].set(jnp.einsum('bixy,ioxy->boxy', x_ft[:, :, -M1:, :M2], w2))
            return jnp.fft.irfft2(out_ft, s=(h, w))
        key = jax.random.key(seed)
        ks = jax.random.split(key, 16)
        scale = 1.0 / (WIDTH * WIDTH)
        d = {'x': jax.random.normal(ks[0], (B, H, W, 3), jnp.float32), 'fc0_w': jax.random.normal(ks[1], (3, WIDTH), jnp.float32) * 0.5, 'fc0_b': jnp.zeros((WIDTH,), jnp.float32), 'ln0_g': jnp.ones((WIDTH,), jnp.float32), 'ln0_b': jnp.zeros((WIDTH,), jnp.float32), 'w1r': jax.random.uniform(ks[2], (LAYERS, WIDTH, WIDTH, M1, M2), jnp.float32) * scale, 'w1i': jax.random.uniform(ks[3], (LAYERS, WIDTH, WIDTH, M1, M2), jnp.float32) * scale, 'w2r': jax.random.uniform(ks[4], (LAYERS, WIDTH, WIDTH, M1, M2), jnp.float32) * scale, 'w2i': jax.random.uniform(ks[5], (LAYERS, WIDTH, WIDTH, M1, M2), jnp.float32) * scale, 'conv_w': jax.random.normal(ks[6], (LAYERS, WIDTH, WIDTH), jnp.float32) * (1.0 / np.sqrt(WIDTH)), 'conv_b': jnp.zeros((LAYERS, WIDTH), jnp.float32), 'ln_g': jnp.ones((LAYERS, WIDTH), jnp.float32), 'ln_b': jnp.zeros((LAYERS, WIDTH), jnp.float32), 'fc1_w': jax.random.normal(ks[7], (WIDTH, 128), jnp.float32) * (1.0 / np.sqrt(WIDTH)), 'fc1_b': jnp.zeros((128,), jnp.float32), 'fc2_w': jax.random.normal(ks[8], (128, 64), jnp.float32) * (1.0 / np.sqrt(128)), 'fc2_b': jnp.zeros((64,), jnp.float32), 'fc3_w': jax.random.normal(ks[9], (64, 1), jnp.float32) * (1.0 / np.sqrt(64)), 'fc3_b': jnp.zeros((1,), jnp.float32)}
        return d
    _L0_tok_all = _L0_tok_setup()
    _L0_tok_in = {k: v for k, v in _L0_tok_all.items() if k in ('fc0_w', 'fc0_b', 'ln0_g', 'ln0_b', 'w1r', 'w1i', 'w2r', 'w2i', 'conv_w', 'conv_b', 'ln_g', 'ln_b', 'fc1_w', 'fc1_b', 'fc2_w', 'fc2_b', 'fc3_w', 'fc3_b')}
    del _L0_tok_all

    def _L0_attn_setup():
        import jax, jax.numpy as jnp
        import numpy as np
        TEMPERATURE = 1.0
        W_BLEND = 0.8
        EPS = 1e-12

        def _l2norm(x):
            n = jnp.sqrt(jnp.sum(x * x, axis=-1, keepdims=True))
            return x / jnp.maximum(n, EPS)
        key = jax.random.key(seed)
        feats = jax.random.normal(key, (4, 512, 64), dtype=jnp.float32)
        return {'feats': feats}
    _L0_attn_all = _L0_attn_setup()
    _L0_attn_in = {k: v for k, v in _L0_attn_all.items() if k in ()}
    del _L0_attn_all

    def _L0_ffn_setup():
        import jax, jax.numpy as jnp
        import numpy as np
        DIM = 64
        HEADS = 8
        NUM_KEYS = 64
        NUM_KV = NUM_KEYS ** 2
        PK_TOPK = 16
        FINAL_TOPK = 16
        DIM_KEY = DIM // 2
        P = 2

        def _pk(x, Wq_pk, pk_keys):
            b, n, _ = x.shape
            q = (x @ Wq_pk).reshape(b, n, P, HEADS, DIM_KEY).transpose(2, 0, 1, 3, 4)
            sim = jnp.einsum('pbnhd,pkhd->pbnhk', q, pk_keys)
            scores, idx = jax.lax.top_k(sim, PK_TOPK)
            idx0 = idx[0]
            idx1 = idx[1] * NUM_KEYS
            index = (idx0[..., :, None] + idx1[..., None, :]).reshape(b, n, HEADS, PK_TOPK * PK_TOPK)
            score = (scores[0][..., :, None] + scores[1][..., None, :]).reshape(b, n, HEADS, PK_TOPK * PK_TOPK)
            final_scores, pk_idx = jax.lax.top_k(score, FINAL_TOPK)
            final_indices = jnp.take_along_axis(index, pk_idx, axis=-1)
            final_scores = jax.nn.softmax(final_scores, axis=-1)
            return (final_scores, final_indices)
        key = jax.random.key(seed)
        ks = jax.random.split(key, 7)
        b, n = (2, 256)
        std = 0.02
        x = jax.random.normal(ks[0], (b, n, DIM), dtype=jnp.float32)
        Wq_pk = jax.random.normal(ks[1], (DIM, P * HEADS * DIM_KEY), dtype=jnp.float32) * std
        pk_keys = jax.random.normal(ks[2], (P, NUM_KEYS, HEADS, DIM_KEY), dtype=jnp.float32) * std
        Wq = jax.random.normal(ks[3], (DIM, HEADS * DIM), dtype=jnp.float32) * std
        keys_table = jax.random.normal(ks[4], (NUM_KV * HEADS, DIM), dtype=jnp.float32) * std
        values_table = jax.random.normal(ks[5], (NUM_KV * HEADS, DIM), dtype=jnp.float32) * std
        Wo = jax.random.normal(ks[6], (DIM * HEADS, DIM), dtype=jnp.float32) * std
        return {'x': x, 'Wq_pk': Wq_pk, 'pk_keys': pk_keys, 'Wq': Wq, 'keys_table': keys_table, 'values_table': values_table, 'Wo': Wo}
    _L0_ffn_all = _L0_ffn_setup()
    _L0_ffn_in = {k: v for k, v in _L0_ffn_all.items() if k in ('Wq_pk', 'pk_keys', 'Wq', 'keys_table', 'values_table', 'Wo')}
    del _L0_ffn_all
    return {'x': x, 'L0_tok_fc0_w': _L0_tok_in['fc0_w'], 'L0_tok_fc0_b': _L0_tok_in['fc0_b'], 'L0_tok_ln0_g': _L0_tok_in['ln0_g'], 'L0_tok_ln0_b': _L0_tok_in['ln0_b'], 'L0_tok_w1r': _L0_tok_in['w1r'], 'L0_tok_w1i': _L0_tok_in['w1i'], 'L0_tok_w2r': _L0_tok_in['w2r'], 'L0_tok_w2i': _L0_tok_in['w2i'], 'L0_tok_conv_w': _L0_tok_in['conv_w'], 'L0_tok_conv_b': _L0_tok_in['conv_b'], 'L0_tok_ln_g': _L0_tok_in['ln_g'], 'L0_tok_ln_b': _L0_tok_in['ln_b'], 'L0_tok_fc1_w': _L0_tok_in['fc1_w'], 'L0_tok_fc1_b': _L0_tok_in['fc1_b'], 'L0_tok_fc2_w': _L0_tok_in['fc2_w'], 'L0_tok_fc2_b': _L0_tok_in['fc2_b'], 'L0_tok_fc3_w': _L0_tok_in['fc3_w'], 'L0_tok_fc3_b': _L0_tok_in['fc3_b'], 'L0_ffn_Wq_pk': _L0_ffn_in['Wq_pk'], 'L0_ffn_pk_keys': _L0_ffn_in['pk_keys'], 'L0_ffn_Wq': _L0_ffn_in['Wq'], 'L0_ffn_keys_table': _L0_ffn_in['keys_table'], 'L0_ffn_values_table': _L0_ffn_in['values_table'], 'L0_ffn_Wo': _L0_ffn_in['Wo']}

def reference(x, L0_tok_fc0_w, L0_tok_fc0_b, L0_tok_ln0_g, L0_tok_ln0_b, L0_tok_w1r, L0_tok_w1i, L0_tok_w2r, L0_tok_w2i, L0_tok_conv_w, L0_tok_conv_b, L0_tok_ln_g, L0_tok_ln_b, L0_tok_fc1_w, L0_tok_fc1_b, L0_tok_fc2_w, L0_tok_fc2_b, L0_tok_fc3_w, L0_tok_fc3_b, L0_ffn_Wq_pk, L0_ffn_pk_keys, L0_ffn_Wq, L0_ffn_keys_table, L0_ffn_values_table, L0_ffn_Wo):
    import jax
    import jax.numpy as jnp

    def _L0_tok_ref(x, fc0_w, fc0_b, ln0_g, ln0_b, w1r, w1i, w2r, w2i, conv_w, conv_b, ln_g, ln_b, fc1_w, fc1_b, fc2_w, fc2_b, fc3_w, fc3_b):
        import jax, jax.numpy as jnp
        import numpy as np
        B, H, W = (16, 64, 64)
        WIDTH, LAYERS, M1, M2 = (32, 4, 12, 12)
        EPS = 1e-05

        def layer_norm(x, g, b):
            mu = jnp.mean(x, axis=-1, keepdims=True)
            var = jnp.mean((x - mu) ** 2, axis=-1, keepdims=True)
            return (x - mu) * jax.lax.rsqrt(var + EPS) * g + b

        def gelu(x):
            return jax.nn.gelu(x, approximate=False)

        def spectral_conv(x, w1, w2):
            b, c, h, w = x.shape
            x_ft = jnp.fft.rfft2(x)
            out_ft = jnp.zeros((b, w1.shape[1], h, w // 2 + 1), dtype=x_ft.dtype)
            out_ft = out_ft.at[:, :, :M1, :M2].set(jnp.einsum('bixy,ioxy->boxy', x_ft[:, :, :M1, :M2], w1))
            out_ft = out_ft.at[:, :, -M1:, :M2].set(jnp.einsum('bixy,ioxy->boxy', x_ft[:, :, -M1:, :M2], w2))
            return jnp.fft.irfft2(out_ft, s=(h, w))
        h = layer_norm(x @ fc0_w + fc0_b, ln0_g, ln0_b)
        h = jnp.transpose(h, (0, 3, 1, 2))
        for i in range(LAYERS):
            w1 = w1r[i] + 1j * w1i[i]
            w2 = w2r[i] + 1j * w2i[i]
            x1 = spectral_conv(h, w1, w2)
            x2 = jnp.einsum('bchw,oc->bohw', h, conv_w[i]) + conv_b[i][None, :, None, None]
            h = x1 + x2
            h = jnp.transpose(h, (0, 2, 3, 1))
            h = layer_norm(h, ln_g[i], ln_b[i])
            if i < LAYERS - 1:
                h = gelu(h)
            h = jnp.transpose(h, (0, 3, 1, 2))
        h = jnp.transpose(h, (0, 2, 3, 1))
        h = gelu(h @ fc1_w + fc1_b)
        h = gelu(h @ fc2_w + fc2_b)
        h = h @ fc3_w + fc3_b
        return h[..., 0]

    def _L0_attn_ref(feats):
        import jax, jax.numpy as jnp
        import numpy as np
        TEMPERATURE = 1.0
        W_BLEND = 0.8
        EPS = 1e-12

        def _l2norm(x):
            n = jnp.sqrt(jnp.sum(x * x, axis=-1, keepdims=True))
            return x / jnp.maximum(n, EPS)
        B, N, C = feats.shape
        f = _l2norm(feats.reshape(B * N, C))
        scores = jnp.matmul(f, f.T) / TEMPERATURE
        attn = jax.nn.softmax(scores, axis=-1)
        feats_att = jnp.matmul(attn, f)
        feats_fcm = f * W_BLEND + feats_att * (1.0 - W_BLEND)
        return _l2norm(feats_fcm.reshape(B, N, C))

    def _L0_ffn_ref(x, Wq_pk, pk_keys, Wq, keys_table, values_table, Wo):
        import jax, jax.numpy as jnp
        import numpy as np
        DIM = 64
        HEADS = 8
        NUM_KEYS = 64
        NUM_KV = NUM_KEYS ** 2
        PK_TOPK = 16
        FINAL_TOPK = 16
        DIM_KEY = DIM // 2
        P = 2

        def _pk(x, Wq_pk, pk_keys):
            b, n, _ = x.shape
            q = (x @ Wq_pk).reshape(b, n, P, HEADS, DIM_KEY).transpose(2, 0, 1, 3, 4)
            sim = jnp.einsum('pbnhd,pkhd->pbnhk', q, pk_keys)
            scores, idx = jax.lax.top_k(sim, PK_TOPK)
            idx0 = idx[0]
            idx1 = idx[1] * NUM_KEYS
            index = (idx0[..., :, None] + idx1[..., None, :]).reshape(b, n, HEADS, PK_TOPK * PK_TOPK)
            score = (scores[0][..., :, None] + scores[1][..., None, :]).reshape(b, n, HEADS, PK_TOPK * PK_TOPK)
            final_scores, pk_idx = jax.lax.top_k(score, FINAL_TOPK)
            final_indices = jnp.take_along_axis(index, pk_idx, axis=-1)
            final_scores = jax.nn.softmax(final_scores, axis=-1)
            return (final_scores, final_indices)
        b, n, d = x.shape
        q = (x @ Wq).reshape(b, n, HEADS, DIM) * DIM ** (-0.5)
        kv_scores, indices = _pk(x, Wq_pk, pk_keys)
        offsets = jnp.arange(HEADS, dtype=indices.dtype) * NUM_KV
        ind = indices + offsets[None, None, :, None]
        k = jnp.einsum('bnhk,bnhkd->bnhd', kv_scores, keys_table[ind])
        v = jnp.einsum('bnhk,bnhkd->bnhd', kv_scores, values_table[ind])
        sim = jnp.einsum('bihd,bjhd->bhij', q, k)
        neg = -jnp.finfo(sim.dtype).max
        causal = jnp.tril(jnp.ones((n, n), dtype=bool))
        sim = jnp.where(causal, sim, neg)
        attn = jax.nn.softmax(sim, axis=-1)
        out = jnp.einsum('bhij,bjhd->bhid', attn, v)
        out = out.transpose(0, 2, 1, 3).reshape(b, n, HEADS * DIM)
        return out @ Wo
    h = _L0_tok_ref(x, L0_tok_fc0_w, L0_tok_fc0_b, L0_tok_ln0_g, L0_tok_ln0_b, L0_tok_w1r, L0_tok_w1i, L0_tok_w2r, L0_tok_w2i, L0_tok_conv_w, L0_tok_conv_b, L0_tok_ln_g, L0_tok_ln_b, L0_tok_fc1_w, L0_tok_fc1_b, L0_tok_fc2_w, L0_tok_fc2_b, L0_tok_fc3_w, L0_tok_fc3_b)
    h = h + _L0_attn_ref(_layernorm(h, axis=-1))
    h = h + _L0_ffn_ref(_layernorm(h, axis=-1), L0_ffn_Wq_pk, L0_ffn_pk_keys, L0_ffn_Wq, L0_ffn_keys_table, L0_ffn_values_table, L0_ffn_Wo)
    return h

_drawn_inputs = setup_inputs


def setup_inputs(seed=0):
    import zlib

    import numpy as np

    out = dict(_drawn_inputs(seed))
    spreads = {'L0_tok_fc0_b': (0.0, 0.1),
     'L0_tok_ln0_g': (1.0, 0.2),
     'L0_tok_ln0_b': (0.0, 0.1),
     'L0_tok_conv_b': (0.0, 0.1),
     'L0_tok_ln_g': (1.0, 0.2),
     'L0_tok_ln_b': (0.0, 0.1),
     'L0_tok_fc1_b': (0.0, 0.1),
     'L0_tok_fc2_b': (0.0, 0.1)}
    factors = {'L0_tok_w1r': 26.296,
     'L0_tok_w1i': 55.062,
     'L0_tok_w2r': 54.532,
     'L0_tok_w2i': 55.81,
     'L0_ffn_Wq_pk': 8.0,
     'L0_ffn_pk_keys': 8.0,
     'L0_ffn_Wq': 64.0,
     'L0_ffn_keys_table': 64.0,
     'L0_ffn_values_table': 8.0,
     'L0_ffn_Wo': 8.0}
    for name, (base, spread) in spreads.items():
        noise = np.random.default_rng([zlib.crc32(name.encode()), seed]).standard_normal(out[name].shape)
        drawn = base * np.exp(spread * noise) if base else spread * noise
        out[name] = jnp.asarray(drawn.astype(out[name].dtype))
    for name, factor in factors.items():
        out[name] = (out[name] * factor).astype(out[name].dtype)
    return out
```

```python
from contextlib import ExitStack

import numpy as np

import concourse.bass as bass
from concourse import mybir

F32 = mybir.dt.float32
I32 = mybir.dt.int32
F32R = mybir.dt.float32r
ACT = mybir.ActivationFunctionType
ALU = mybir.AluOpType
AX = mybir.AxisListType

IMAGES, H, W = 128, 64, 64
C, LAYERS, M1, M2 = 32, 4, 12, 12
QI = 4
QUADS = IMAGES // QI
PX = H * W
TILES = PX // 128
GROUPS = TILES // 4
ROWS = 2 * 2 * M1
EPS = 1e-5
ROOT_GUESS = 1597463007.0
ROOT_STEPS = 11


def shape_constants():
    r2, w = np.arange(2), np.arange(W)
    ky, h = np.arange(M2), np.arange(H)
    phi = 2 * np.pi * np.outer(w, ky) / W
    f1 = np.zeros((2, W, 2, M2, 2))
    for r in r2:
        f1[r, :, r, :, 0] = np.cos(phi)
        f1[r, :, r, :, 1] = -np.sin(phi)
    freq = np.stack([np.arange(M1), np.arange(H - M1, H)], 1)
    th = 2 * np.pi * h[:, None, None] * freq[None] / H
    g = np.zeros((H, 2, M1, 2, 2))
    g[:, 0, :, :, 0] = np.cos(th)
    g[:, 1, :, :, 0] = np.sin(th)
    g[:, 0, :, :, 1] = -np.sin(th)
    g[:, 1, :, :, 1] = np.cos(th)
    gi = np.zeros((M1, 2, 2, H, 2))
    tt = th.transpose(1, 2, 0)
    gi[:, :, 0, :, 0] = np.cos(tt)
    gi[:, :, 1, :, 0] = -np.sin(tt)
    gi[:, :, 0, :, 1] = np.sin(tt)
    gi[:, :, 1, :, 1] = np.cos(tt)
    weight = np.where(ky == 0, 1.0, 2.0)[:, None] / (H * W)
    e = np.zeros((97, 2, 2, W))
    ev = e[:96].reshape(4, M2, 2, 2, 2, W)
    for par in range(2):
        for r in r2:
            ev[2 * par + r, :, 0, par, r] = weight * np.cos(phi.T)
            ev[2 * par + r, :, 1, par, r] = -weight * np.sin(phi.T)
    e[96] = 1.0
    centre = np.kron(np.eye(4), np.eye(C) - 1.0 / C)
    block = np.kron(np.eye(4), np.ones((C, C)))
    fc0 = np.zeros((97, 2, 4, 4))
    fv = fc0[:96].reshape(8, 4, 3, 2, 4, 4)
    for j in range(8):
        for i in range(4):
            fv[j, i, :, j % 2, j // 2, i] = 1.0
    fc0[96] = 1.0
    pos = np.arange(128)
    causal = np.where((pos[:, None] // 64 == pos[None] // 64) & (pos[None] <= pos[:, None]), 0.0, -1e30)
    f = lambda a, n: np.ascontiguousarray(a.reshape(n, -1), dtype=np.float32)
    return {"k_f1": f(f1, 128), "k_g": f(g, 128), "k_gi": f(gi, ROWS), "k_e": f(e, 97), "k_ident": f(np.eye(128), 128),
            "k_centre": f(centre, 128), "k_block": f(block, 128), "k_fc0": f(fc0, 97), "k_causal": f(causal, 128)}


class Quad:

    def __init__(self, half, parity, fixed):
        self.half, self.parity, self.fixed = half, parity, fixed

    @property
    def n(self):
        return self.half * 2 + self.parity

    def __add__(self, d):
        carry, parity = divmod(self.parity + d, 2)
        return Quad(self.half + carry, parity, self.fixed)

    def uses(self, before):
        return self.half + (1 - before // 2)

    @property
    def exists(self):
        return not self.fixed or 0 <= self.n < QUADS

    def back(self, slot, lag, period=GROUPS):
        d, unit = divmod(slot - lag, period)
        return self + d, unit


def quad_times(eng, body, first=-1, last=QUADS + 2):
    for n in range(first, 2):
        body(Quad(n // 2, n % 2, True))
    with eng.Fori(1, QUADS // 2 - 1) as pair:
        for u in range(2):
            body(Quad(pair, u, False))
    for n in range(QUADS - 2, last):
        body(Quad(n // 2, n % 2, True))


def forward_units(q, s):
    early, middle, late = {}, {0: 1, 2: 2, 4: 3}, {4: 4, 5: 7}
    early.update({5: 5, 6: 8})
    middle.update({5: 6, 6: 9})
    places = [[(q + -1, units[s])] if s in units else [] for units in (early, middle, late)]
    if s == 6:
        places[2].append((q, 0))
    return places


def wait(eng, sem, value):
    if not isinstance(value, int) or value > 0:
        eng.wait_ge(sem, value)


def tile_of(g, t):
    return 8 * (g // 2) + 2 * t + g % 2


class Store:

    def __init__(self, nc, ctx, prefix):
        self.nc, self.ctx, self.prefix = nc, ctx, prefix
        self.sems = []
        ctx.callback(self.release)

    def release(self):
        self.nc.clear_and_free_semaphores(self.sems)
        self.nc.all_engine_barrier()

    def sb(self, name, shape, dtype=F32):
        return self.ctx.enter_context(self.nc.sbuf_tensor(f"{self.prefix}_{name}", shape, dtype))

    def ps(self, name, shape):
        return self.ctx.enter_context(self.nc.psum_tensor(f"{self.prefix}_{name}", shape, F32))

    def sem(self, name):
        self.sems.append(self.nc.alloc_semaphore(f"{self.prefix}_{name}"))
        return self.sems[-1]


def tower_pass(nc, layer, T):
    first, final = layer < 0, layer == LAYERS - 1
    fwd = not final
    ZU = 2 if first else 7
    FU = 10
    with ExitStack() as ctx:
        m = Store(nc, ctx, f"p{layer + 1}")
        ident = m.sb("ident", [128, 128])
        gain = m.sb("gain", [128, 1])
        shift = m.sb("shift", [128, 1])
        BATCH = 1 if final else 2
        ssq = m.sb("ssq", [128, 2, BATCH * 16])
        rstd = m.sb("rstd", [128, 2, BATCH * 16])
        newton = m.sb("newton", [128, BATCH * 16])
        square = m.sb("square", [128, 2, 512])
        normed = m.sb("normed", [128, 2, 512])
        if first:
            xs = m.sb("xs", [128, 2, 128, 3])
            xb = m.sb("xb", [128, TILES, QI, 3])
            xt = m.sb("xt", [97, 2, 4, 128])
            fc0 = m.sb("fc0", [97, 32, C])
            mask = m.sb("mask", [97, 32])
            fc0w = m.sb("fc0w", [97, C])
            fc0sum = m.sb("fc0sum", [97, 1])
            fc0mean = m.sb("fc0mean", [97, 1])
            fc0c = m.sb("fc0c", [97, C])
        else:
            hin = m.sb("hin", [128, 2, PX])
            yq = m.sb("yq", [ROWS, 2, M2, 128])
            z1 = m.sb("z1", [128, H, M2, 2])
            z2 = m.sb("z2", [97, 2, 16, 128])
            gi = m.sb("gi", [ROWS, 128])
            emat = m.sb("emat", [97, 2, 128])
            centre = m.sb("centre", [128, 128])
            block = m.sb("block", [128, 4, C])
            convrow = m.sb("convrow", [128, C])
            convdiag = m.sb("convdiag", [128, 4, C])
            wconv = m.sb("wconv", [128, 128])
            biascol = m.sb("biascol", [128, 97])
        NACC = 2 if final else 4
        accs = [m.ps(f"acc{k}", [128, 512]) for k in range(NACC)]
        ta = m.ps("ta", [128, 512])
        zbank = m.ps("zbank", [128, 512])
        if fwd:
            hout = m.sb("hout", [128, 2, PX])
            hb = m.sb("hb", [128, 2, 8, 128])
            a1 = m.sb("a1", [128, M2, H, 2])
            a2 = m.sb("a2", [128, M2, 128])
            xq = m.sb("xq", [ROWS, 2, M2, 128])
            f1 = m.sb("f1", [128, 48])
            gm = m.sb("gm", [128, ROWS])
            tb = m.ps("tb", [128, 512])
            fbank = m.ps("fbank", [128, 512])
        else:
            hln = m.sb("hln", [128, 2, 512])
            g1 = m.sb("g1", [128, 2, 2, 512])
            g2 = m.sb("g2", [128, 2, 512])
            w1 = m.sb("w1", [128, 128])
            b1 = m.sb("b1", [128, 1])
            w2 = m.sb("w2", [128, 64])
            b2 = m.sb("b2", [128, 1])
            w3 = m.sb("w3", [128, 2])
            b3 = m.sb("b3", [128, 1])
            o1 = m.sb("o1", [128, 128])
            o2 = m.sb("o2", [128, 2, 128])
            fc1p = m.ps("fc1p", [128, 2, 512])
            fc2p = m.ps("fc2p", [128, 512])
            fc3p = m.ps("fc3p", [128, 512])

        consts_in, zeroed, prepared = m.sem("consts_in"), m.sem("zeroed"), m.sem("prepared")
        conv_made = m.sem("conv_made")
        in_loaded = [m.sem(f"in_loaded{k}") for k in range(2)]
        y_loaded = [m.sem(f"y_loaded{k}") for k in range(2)]
        z_made, z_copied = m.sem("z_made"), m.sem("z_copied")
        acc_made, squared, summed = m.sem("acc_made"), m.sem("squared"), m.sem("summed")
        root_step, norm_made = m.sem("root_step"), m.sem("norm_made")
        ta_made, ln_made = m.sem("ta_made"), m.sem("ln_made")
        if fwd:
            tb_made, hb_copied = m.sem("tb_made"), m.sem("hb_copied")
            f_made, f_copied = m.sem("f_made"), m.sem("f_copied")
            h_stored = [m.sem(f"h_stored{k}") for k in range(2)]
            x_stored = [m.sem(f"x_stored{k}") for k in range(2)]
        else:
            fc1_made, fc1_gelu = m.sem("fc1_made"), m.sem("fc1_gelu")
            fc2_made, fc2_gelu = m.sem("fc2_made"), m.sem("fc2_gelu")
            fc3_made, out_biased = m.sem("fc3_made"), m.sem("out_biased")
            out_turned, out_copied = m.sem("out_turned"), m.sem("out_copied")
            out_stored = [m.sem(f"out_stored{k}") for k in range(2)]

        hsrc, hdst = T["h"][(layer + 1) % 2], T["h"][layer % 2]
        column = lambda v: v.rearrange("(c o) -> c o", o=1)
        loads, late_loads = [(ident[:, :], T["k_ident"])], []
        lng, lnb = (T["ln0_g"], T["ln0_b"]) if first else (T["ln_g"][layer], T["ln_b"][layer])
        for i in range(QI):
            loads += [(gain[C * i:C * i + C, :], column(lng)), (shift[C * i:C * i + C, :], column(lnb))]
        if first:
            loads += [(fc0w[3 * j:3 * j + 3, :], T["fc0_w"]) for j in range(32)]
            loads += [(fc0w[96:97, :], T["fc0_b"].rearrange("(o c) -> o c", o=1)), (mask[:, :], T["k_fc0"])]
        else:
            loads += [(gi[:, :], T["k_gi"]), (emat[:, :, :].rearrange("p a b -> p (a b)"), T["k_e"]),
                      (centre[:, :], T["k_centre"]), (block[:, :, :].rearrange("p a b -> p (a b)"), T["k_block"])]
            loads += [(convrow[C * i:C * i + C, :], T["conv_w"][layer]) for i in range(QI)]
            late_loads += [(biascol[C * i:C * i + C, 96:97], column(T["conv_b"][layer])) for i in range(QI)]
        if fwd:
            loads += [(f1[:, :], T["k_f1"]), (gm[:, :], T["k_g"])]
        else:
            loads += [(w1[C * i:C * i + C, :], T["fc1_w"]) for i in range(QI)]
            loads += [(b1[:, :], column(T["fc1_b"])), (w2[:, :], T["fc2_w"]),
                      (b3[:, :], T["fc3_b"].rearrange("(o c) -> o c", o=1).broadcast_to([128, 1]))]
            loads += [(b2[64 * i:64 * i + 64, :], column(T["fc2_b"])) for i in range(2)]
            late_loads += [(w3[64 * i:64 * i + 64, i:i + 1], T["fc3_w"]) for i in range(2)]
        ALL_IN = 16 * (len(loads) + len(late_loads))
        NPREP = 5
        unit = lambda q, g: q.n * GROUPS + g

        with nc.Block() as blk:
            @blk.sync
            def _(sp):
                for dst, src in loads:
                    sp.dma_start(dst, src).then_inc(consts_in, 16)
                sp.wait_ge(zeroed, 2 if final else 1)
                for dst, src in late_loads:
                    sp.dma_start(dst, src).then_inc(consts_in, 16)

                def load_in(q):
                    if not q.exists:
                        return
                    if first:
                        wait(sp, z_made, (q.n - 2) * ZU + 1)
                        sp.dma_start(xs[:, q.parity, :, :].rearrange("p a b -> p (a b)"), T["x"][q.n]).then_inc(in_loaded[q.parity], 16)
                    else:
                        wait(sp, acc_made, (q.n - 2) * GROUPS + GROUPS)
                        sp.dma_start(hin[:, q.parity, :], hsrc[q.n]).then_inc(in_loaded[q.parity], 16)

                def load_y(q):
                    if not first and q.exists:
                        wait(sp, z_made, (q.n - 2) * ZU + 3)
                        sp.dma_start(yq[:, q.parity, :, :], T["Y"][q.n]).then_inc(y_loaded[q.parity], 16)

                def body(q):
                    if first:
                        load_in(q + 1)
                    else:
                        load_in(q)
                    load_y(q + 1)

                quad_times(sp, body, last=QUADS)

            @blk.gpsimd
            def _(pool):
                fills = [(xt[96:97, :, :, :], 1.0) if first else (biascol[:, :], 0.0)]
                fills += [(w3[:, :], 0.0)] if final else []
                for n, (dst, value) in enumerate(fills):
                    pool.memset(dst, value).then_inc(zeroed, 1)
                    pool.wait_ge(zeroed, n + 1)

            @blk.vector
            def _(dve):
                dve.wait_ge(consts_in, ALL_IN)
                dve.tensor_scalar(gain[:, :], gain[:, :], float(C) ** 0.5, None, ALU.mult).then_inc(prepared, 1)
                if first:
                    dve.tensor_reduce(fc0sum[:, :], fc0w[:, :], AX.X, ALU.add).then_inc(prepared, 1)
                    dve.wait_ge(prepared, 2)
                    dve.tensor_scalar(fc0mean[:, :], fc0sum[:, :], 1.0 / C, None, ALU.mult).then_inc(prepared, 1)
                    dve.wait_ge(prepared, 3)
                    dve.tensor_scalar(fc0c[:, :], fc0w[:, :], fc0mean[:, 0:1], None, ALU.subtract).then_inc(prepared, 1)
                    dve.wait_ge(prepared, 4)
                    dve.tensor_tensor(fc0[:, :, :], mask[:, :].unsqueeze(2).broadcast_to([97, 32, C]),
                                      fc0c[:, :].unsqueeze(1).broadcast_to([97, 32, C]), ALU.mult).then_inc(prepared, 1)
                else:
                    dve.tensor_tensor(convdiag[:, :, :], block[:, :, :],
                                      convrow[:, :].unsqueeze(1).broadcast_to([128, 4, C]), ALU.mult).then_inc(prepared, 1)
                    dve.wait_ge(conv_made, 1)
                    dve.tensor_copy(wconv[:, :], accs[0][:, 0:128]).then_inc(prepared, 1)
                    for p in range(2):
                        dve.tensor_copy(z2[96:97, p, :, :], accs[1][96:97, 0:128].unsqueeze(1).broadcast_to([1, 16, 128])).then_inc(prepared, 1)

                def sums(q, g):
                    if q.exists:
                        at = 16 * (g % BATCH)
                        wait(dve, squared, unit(q, g) + 1)
                        dve.tensor_reduce(ssq[:, (g // BATCH) % 2, at:at + 16], square[:, g % 2, :].rearrange("p (n c) -> p n c", c=C), AX.X,
                                          ALU.add).then_inc(summed, 1)

                def roots(q, b):
                    if not q.exists:
                        return
                    v, y = ssq[:, b % 2, :], rstd[:, b % 2, :]
                    done = (q.n * (GROUPS // BATCH) + b) * ROOT_STEPS
                    wait(dve, summed, unit(q, b * BATCH) + BATCH)
                    dve.tensor_scalar(v, v, C * EPS, None, ALU.add).then_inc(root_step, 1)
                    dve.wait_ge(root_step, done + 1)
                    dve.tensor_scalar(y.bitcast(I32), v.bitcast(I32), -0.5, ROOT_GUESS, ALU.mult, ALU.add).then_inc(root_step, 1)
                    for k in range(2, ROOT_STEPS, 3):
                        dve.wait_ge(root_step, done + k)
                        dve.scalar_tensor_tensor(out=newton[:, :], in0=y, scalar=-0.5, in1=y, op0=ALU.mult, op1=ALU.mult).then_inc(root_step, 1)
                        dve.wait_ge(root_step, done + k + 1)
                        dve.tensor_tensor(newton[:, :], newton[:, :], v, ALU.mult).then_inc(root_step, 1)
                        dve.wait_ge(root_step, done + k + 2)
                        dve.scalar_tensor_tensor(out=y, in0=newton[:, :], scalar=1.5, in1=y, op0=ALU.add, op1=ALU.mult).then_inc(root_step, 1)

                def normalise(q, g):
                    if q.exists:
                        b, at = g // BATCH, 16 * (g % BATCH)
                        if g % BATCH == 0:
                            wait(dve, root_step, (q.n * (GROUPS // BATCH) + b + 1) * ROOT_STEPS)
                        wait(dve, ta_made, unit(q, g) - 1)
                        dve.tensor_tensor(normed[:, g % 2, :].rearrange("p (n c) -> p n c", c=C),
                                          accs[g % NACC][:, :].rearrange("p (n c) -> p n c", c=C),
                                          rstd[:, b % 2, at:at + 16].unsqueeze(2).broadcast_to([128, 16, C]), ALU.mult).then_inc(norm_made, 1)

                def copy_hb(q, g):
                    if q.exists:
                        wait(dve, tb_made, unit(q, g) + 1)
                        wait(dve, f_made, q.n * FU + g // 2 - 1 if g >= 4 else (q.n - 1) * FU + g // 2 + 3)
                        dve.tensor_copy(hb[:, (g // 2) % 2, g % 2::2, :], tb[:, :].rearrange("p (t n) -> p t n", t=4)).then_inc(hb_copied, 1)

                def finish(q):
                    if q.exists:
                        wait(dve, fc3_made, q.n * GROUPS + GROUPS)
                        wait(dve, out_turned, q.n)
                        dve.tensor_scalar(o1[:, :], fc3p[:, 0:128], b3[:, 0:1], None, ALU.add).then_inc(out_biased, 1)

                def out_copy(q):
                    if q.exists:
                        wait(dve, out_turned, q.n + 1)
                        stored(dve, out_stored, q, 2)
                        dve.tensor_copy(o2[:, q.parity, :], fc3p[:, 256:384]).then_inc(out_copied, 1)

                def body(q):
                    for s in range(GROUPS):
                        if fwd:
                            copy_hb(*q.back(s, 5))
                            normalise(*q.back(s, 2))
                            sums(q, s)
                            if s % 2 == 1:
                                roots(q, s // 2)
                        else:
                            normalise(*q.back(s, 1))
                            sums(q, s)
                            roots(q, s)
                        if final and s == 4:
                            finish(q + -1)
                        if final and s == 4:
                            out_copy(q + -1)

                quad_times(dve, body, first=0)

            @blk.scalar
            def _(act):
                copy = lambda dst, src: act.activation(dst, src, ACT.Copy)

                def squares(q, g):
                    if q.exists:
                        wait(act, acc_made, unit(q, g) + 1)
                        wait(act, summed, unit(q, g) - 1)
                        act.activation(square[:, g % 2, :], accs[g % NACC][:, :], ACT.Square).then_inc(squared, 1)

                def affine(q, g):
                    if not q.exists:
                        return
                    wait(act, ta_made, unit(q, g) + 1)
                    if fwd:
                        if g == 0:
                            stored(act, h_stored, q, 2)
                            wait(act, tb_made, (q.n - 1) * GROUPS)
                        at = 8 * (g // 2)
                        dst = hout[:, q.parity, at * 128:(at + 8) * 128].rearrange("p (t r n) -> p t r n", r=2, n=128)[:, :, g % 2, :]
                        src = ta[:, :].rearrange("p (t n) -> p t n", t=4)
                    else:
                        wait(act, fc1_made, (unit(q, g) - 1) * 2)
                        dst, src = hln[:, g % 2, :], ta[:, :]
                    fn = ACT.Identity if first or final else ACT.Gelu
                    act.activation(dst, src, fn, bias=shift[:, 0:1], scale=gain[:, 0:1]).then_inc(ln_made, 1)

                def z_copy(q, k):
                    if not q.exists or k >= ZU:
                        return
                    wait(act, z_made, q.n * ZU + k + 1)
                    if first and k == 0:
                        wait(act, z_made, q.n * ZU)
                        copy(xb[:, :, :, :].rearrange("p j i ch -> p ch i j"),
                             zbank[:, 0:384].rearrange("p (ch i j) -> p ch i j", ch=3, i=QI)).then_inc(z_copied, 1)
                    elif first and k == 1:
                        wait(act, acc_made, (q.n - 1) * GROUPS)
                        copy(xt[0:96, q.parity, :, :], zbank[0:96, :].rearrange("p (b n) -> p b n", b=4)).then_inc(z_copied, 1)
                    elif k < 3:
                        copy(z1[:, :, 4 * k:4 * k + 4, :].rearrange("p h k r -> p k h r"),
                             zbank[:, :].rearrange("p (k h r) -> p k h r", k=4, r=2)).then_inc(z_copied, 1)
                    else:
                        wait(act, acc_made, (q.n - 1) * GROUPS)
                        copy(z2[0:96, q.parity, 4 * (k - 3):4 * (k - 3) + 4, :],
                             zbank[0:96, :].rearrange("p (b n) -> p b n", b=4)).then_inc(z_copied, 1)

                def f_copy(q, k):
                    if not q.exists:
                        return
                    wait(act, f_made, q.n * FU + k + 1)
                    if k < 4:
                        copy(a1[:, :, 16 * k:16 * k + 16, :].rearrange("p k h r -> p h k r"),
                             fbank[:, 0:384].rearrange("p (h k r) -> p h k r", k=M2, r=2)).then_inc(f_copied, 1)
                    elif k < 7:
                        copy(a2[:, 4 * (k - 4):4 * (k - 4) + 4, :].rearrange("p k n -> p (k n)"), fbank[:, :]).then_inc(f_copied, 1)
                    else:
                        if k == 7:
                            stored(act, x_stored, q, 2)
                        copy(xq[:, q.parity, 4 * (k - 7):4 * (k - 7) + 4, :].rearrange("p k n -> p (k n)"),
                             fbank[0:ROWS, :]).then_inc(f_copied, 1)
                        if k == FU - 1:
                            wait(act, f_copied, q.n * FU + FU)
                            act.dma_start(T["X"][q.n], xq[:, q.parity, :, :]).then_inc(x_stored[q.parity], 16)

                def store_h(q):
                    if q.exists:
                        wait(act, ln_made, q.n * GROUPS + GROUPS)
                        act.dma_start(hdst[q.n], hout[:, q.parity, :]).then_inc(h_stored[q.parity], 16)

                def gelu1(q, g, pair):
                    if q.exists:
                        n = unit(q, g) * 2 + pair
                        wait(act, fc1_made, n + 1)
                        wait(act, fc2_made, n - 1)
                        act.activation(g1[:, pair, :, :], fc1p[:, :, :], ACT.Gelu, bias=b1[:, 0:1]).then_inc(fc1_gelu, 1)

                def gelu2(q, g, pair):
                    if q.exists:
                        wait(act, fc2_made, unit(q, g) * 2 + pair + 1)
                        wait(act, fc3_made, unit(q, g))
                        act.activation(g2[:, pair, :], fc2p[:, :], ACT.Gelu, bias=b2[:, 0:1]).then_inc(fc2_gelu, 1)

                def store_out(q):
                    if q.exists:
                        wait(act, out_copied, q.n + 1)
                        act.dma_start(T["tok"][q.n], o2[:, q.parity, :]).then_inc(out_stored[q.parity], 16)

                def body(q):
                    for s in range(GROUPS):
                        if final:
                            gelu1(*q.back(s, 3), 0)
                            squares(q, s)
                            gelu1(*q.back(s, 3), 1)
                            gelu2(*q.back(s, 3), 0)
                            z_copy(q + 1, s)
                            affine(*q.back(s, 2))
                            gelu2(*q.back(s, 3), 1)
                            if s == 7:
                                store_out(q + -1)
                            continue
                        early, middle, late = forward_units(q, s)
                        squares(q, s)
                        for unit_at in early:
                            f_copy(*unit_at)
                        z_copy(q + 1, s)
                        affine(*q.back(s, 3))
                        if s == 3:
                            store_h(q + -1)
                        for unit_at in middle + late:
                            f_copy(*unit_at)

                act.wait_ge(prepared, NPREP)
                act.wait_ge(consts_in, ALL_IN)
                quad_times(act, body)
                for p in range(2):
                    for sem in ((h_stored[p], x_stored[p]) if fwd else (out_stored[p],)):
                        act.wait_ge(sem, 16 * QUADS // 2)

            @blk.tensor
            def _(pe):
                pe.wait_ge(consts_in, ALL_IN)
                pe.wait_ge(zeroed, 2 if final else 1)
                if not first:
                    pe.wait_ge(prepared, 2)
                    pe.matmul(accs[0][:, 0:128], convdiag[:, :, :].rearrange("p a b -> p (a b)"), centre[:, :], start=True, stop=True)
                    pe.matmul(accs[1][0:97, 0:128], biascol[:, :], centre[:, :], start=True, stop=True).then_inc(conv_made, 1)
                pe.wait_ge(prepared, NPREP)

                def prepare(q, k):
                    if not q.exists or k >= ZU:
                        return
                    wait(pe, z_copied, q.n * ZU + k)
                    if first and k == 0:
                        loaded(pe, in_loaded, q)
                        for ch in range(3):
                            mm = pe.transpose(zbank[:, 128 * ch:128 * ch + 128], xs[:, q.parity, :, ch], ident[:, :])
                    elif first and k == 1:
                        for b in range(4):
                            mm = pe.transpose(zbank[0:96, 128 * b:128 * b + 128],
                                              xb[:, 8 * b:8 * b + 8, :, :].rearrange("p j i ch -> p (j i ch)"), ident[:, :])
                    elif k < 3:
                        if k == 0:
                            loaded(pe, y_loaded, q)
                        for d in range(4):
                            mm = pe.matmul(zbank[:, 128 * d:128 * d + 128], yq[:, q.parity, 4 * k + d, :], gi[:, :], start=True, stop=True)
                    else:
                        for d in range(4):
                            b = 4 * (k - 3) + d
                            mm = pe.transpose(zbank[0:96, 128 * d:128 * d + 128],
                                              z1[:, 4 * b:4 * b + 4, :, :].rearrange("p h k r -> p (h k r)"), ident[:, :])
                    mm.then_inc(z_made, 1)

                def accumulate(q, g):
                    if not q.exists:
                        return
                    acc = accs[g % NACC]
                    wait(pe, norm_made, unit(q, g) - NACC + 1)
                    if first:
                        wait(pe, z_copied, q.n * ZU + 2)
                        cols = fc0[:, 16 * (g % 2):16 * (g % 2) + 16, :].rearrange("p n c -> p (n c)")
                        mm = pe.matmul(acc[:, :], xt[:, q.parity, g // 2, :], cols, start=True, stop=True)
                    else:
                        if g == 0:
                            loaded(pe, in_loaded, q)
                            wait(pe, z_copied, q.n * ZU + ZU)
                        gg, par = g // 2, g % 2
                        pe.matmul(acc[:, :], emat[:, par, :], z2[:, q.parity, 4 * gg:4 * gg + 4, :].rearrange("p b n -> p (b n)"),
                                  start=True, stop=False)
                        for t in range(4):
                            j = tile_of(g, t)
                            mm = pe.matmul(acc[:, 128 * t:128 * t + 128], hin[:, q.parity, 128 * j:128 * j + 128], wconv[:, :],
                                           start=False, stop=(t == 3))
                    mm.then_inc(acc_made, 1)

                def to_channels(q, g):
                    if q.exists:
                        wait(pe, norm_made, unit(q, g) + 1)
                        wait(pe, ln_made, unit(q, g))
                        for t in range(4):
                            mm = pe.transpose(ta[:, 128 * t:128 * t + 128], normed[:, g % 2, 128 * t:128 * t + 128], ident[:, :])
                        mm.then_inc(ta_made, 1)

                def to_pixels(q, g):
                    if q.exists:
                        wait(pe, ln_made, unit(q, g) + 1)
                        wait(pe, hb_copied, unit(q, g))
                        for t in range(4):
                            j = tile_of(g, t)
                            mm = pe.transpose(tb[:, 128 * t:128 * t + 128], hout[:, q.parity, 128 * j:128 * j + 128], ident[:, :])
                        mm.then_inc(tb_made, 1)

                def forward(q, k):
                    if not q.exists:
                        return
                    wait(pe, f_copied, q.n * FU + k)
                    if k < 4:
                        wait(pe, hb_copied, q.n * GROUPS + 2 * k + 2)
                        for j in range(8):
                            mm = pe.matmul(fbank[:, 48 * j:48 * j + 48], hb[:, k % 2, j, :], f1[:, :], start=True, stop=True)
                    elif k < 7:
                        for d in range(4):
                            mm = pe.transpose(fbank[:, 128 * d:128 * d + 128], a1[:, 4 * (k - 4) + d, :, :].rearrange("p h r -> p (h r)"), ident[:, :])
                    else:
                        at = 4 * (k - 7)
                        mm = pe.matmul(fbank[0:ROWS, :], gm[:, :], a2[:, at:at + 4, :].rearrange("p k n -> p (k n)"), start=True, stop=True)
                    mm.then_inc(f_made, 1)

                def fc1(q, g, pair):
                    if q.exists:
                        n = unit(q, g) * 2 + pair
                        wait(pe, ln_made, unit(q, g) + 1)
                        wait(pe, fc1_gelu, n)
                        for e in range(2):
                            i = 2 * pair + e
                            mm = pe.matmul(fc1p[:, e, :], w1[C * i:C * i + C, :], hln[C * i:C * i + C, g % 2, :], start=True, stop=True)
                        mm.then_inc(fc1_made, 1)

                def fc2(q, g, pair):
                    if q.exists:
                        n = unit(q, g) * 2 + pair
                        wait(pe, fc1_gelu, n + 1)
                        wait(pe, fc2_gelu, n)
                        for e in range(2):
                            mm = pe.matmul(fc2p[64 * e:64 * e + 64, :], w2[:, :], g1[:, pair, e, :], start=True, stop=True)
                        mm.then_inc(fc2_made, 1)

                def fc3(q, g):
                    if q.exists:
                        wait(pe, fc2_gelu, unit(q, g) * 2 + 2)
                        if g == 0:
                            wait(pe, out_copied, q.n)
                        for pair in range(2):
                            for t in range(4):
                                col = 64 * pair + tile_of(g, t)
                                mm = pe.matmul(fc3p[:, col:col + 33:32], g2[:, pair, 128 * t:128 * t + 128], w3[:, :], start=True, stop=True)
                        mm.then_inc(fc3_made, 1)

                def turn_out(q):
                    if q.exists:
                        wait(pe, out_biased, q.n + 1)
                        wait(pe, out_copied, q.n)
                        pe.transpose(fc3p[:, 256:384], o1[:, :], ident[:, :]).then_inc(out_turned, 1)

                def body(q):
                    for s in range(GROUPS):
                        if final:
                            fc1(*q.back(s, 3), 0)
                            accumulate(q, s)
                            if s == 4:
                                turn_out(q + -1)
                            fc3(*q.back(s, 4))
                            fc1(*q.back(s, 3), 1)
                            fc2(*q.back(s, 3), 0)
                            prepare(q + 1, s)
                            to_channels(*q.back(s, 2))
                            fc2(*q.back(s, 3), 1)
                            continue
                        early, middle, late = forward_units(q, s)
                        accumulate(q, s)
                        for unit_at in early:
                            forward(*unit_at)
                        prepare(q + 1, s)
                        to_channels(*q.back(s, 3))
                        for unit_at in middle:
                            forward(*unit_at)
                        to_pixels(*q.back(s, 4))
                        for unit_at in late:
                            forward(*unit_at)

                quad_times(pe, body)


def loaded(eng, sems, q):
    eng.wait_ge(sems[q.parity], q.uses(0) * 16)


def stored(eng, sems, q, before):
    wait(eng, sems[q.parity], q.uses(before) * 16)


def mix_pass(nc, layer, T):
    with ExitStack() as ctx:
        m = Store(nc, ctx, f"m{layer}")
        ident = m.sb("ident", [128, 128])
        raw = m.sb("raw", [128, 2, C, M1 * M2])
        mean = m.sb("mean", [128, 2, M1 * M2])
        wk = m.sb("wk", [128, 2, M1, 2, C])
        xi = m.sb("xi", [128, 2, M1, 128])
        xt = m.sb("xt", [128, M1, 128])
        yo = m.sb("yo", [128, 2, M1, 2, 64])
        turned = m.ps("turned", [128, 3, 512])
        prod = [m.ps(f"prod{s}", [128, 2, 512]) for s in range(2)]
        consts_in, negated, summed, centred = m.sem("consts_in"), m.sem("negated"), m.sem("summed"), m.sem("centred")
        x_in = [m.sem(f"x_in{k}") for k in range(2)]
        y_out = [m.sem(f"y_out{k}") for k in range(2)]
        w_cut, x_turned, x_copied = m.sem("w_cut"), m.sem("x_turned"), m.sem("x_copied")
        mixed, y_copied = m.sem("mixed"), m.sem("y_copied")
        flat = raw[:, :, :, :].rearrange("p r c m -> p r (c m)")
        with nc.Block() as blk:
            @blk.sync
            def _(sp):
                sp.dma_start(ident[:, :], T["k_ident"]).then_inc(consts_in, 16)
                for side, (wr, wi) in enumerate((("w1r", "w1i"), ("w2r", "w2i"))):
                    for rin in range(2):
                        p = 64 * side + 32 * rin
                        for rout in range(2):
                            src = T[wi if rin != rout else wr][layer].rearrange("i o x y -> i (o x y)")
                            sp.dma_start(flat[p:p + 32, rout, :], src).then_inc(consts_in, 16)
                with sp.Fori(0, M2 // 2) as i:
                    for u in range(2):
                        sp.wait_ge(x_turned, i * 2 + u + 1)
                        sp.dma_start(xi[:, u, :, :].rearrange("p k n -> p (k n)").rearrange("p (r c) -> p r c", c=C),
                                     T["Xk"][i * 2 + u]).then_inc(x_in[u], 16)

            @blk.gpsimd
            def _(pool):
                pool.wait_ge(centred, 2)
                with pool.Fori(0, M2 // 2) as i:
                    for u in range(2):
                        ky = i * 2 + u
                        pool.wait_ge(mixed, ky + 1)
                        pool.tensor_copy(wk[:, u, :, :, :],
                                         raw[:, :, :, :].rearrange("p r c (x y) -> p x r c y", y=M2)[:, :, :, :, bass.ds(ky, 1)].rearrange("p x r c y -> p x r (c y)")).then_inc(w_cut, 1)

            @blk.vector
            def _(dve):
                dve.wait_ge(consts_in, 16 * 9)
                for side in range(2):
                    p = 64 * side + 32
                    mm = dve.tensor_scalar(flat[p:p + 32, 0, :], flat[p:p + 32, 0, :], -1.0, None, ALU.mult)
                    mm.then_inc(negated, 1)
                dve.wait_ge(negated, 2)
                dve.tensor_reduce(mean[:, :, :], raw[:, :, :, :].rearrange("p r c m -> p r m c"), AX.X, ALU.add).then_inc(summed, 1)
                dve.wait_ge(summed, 1)
                for rout in range(2):
                    dve.scalar_tensor_tensor(out=raw[:, rout, :, :], in0=mean[:, rout, :].unsqueeze(1).broadcast_to([128, C, M1 * M2]),
                                             scalar=-1.0 / C, in1=raw[:, rout, :, :], op0=ALU.mult, op1=ALU.add).then_inc(centred, 1)
                with dve.Fori(0, M2 // 2) as i:
                    for u in range(2):
                        ky = i * 2 + u
                        for b in range(3):
                            dve.wait_ge(x_turned, ky + 3)
                            mm = dve.tensor_copy(xt[:, 4 * b:4 * b + 4, :].rearrange("p k n -> p (k n)"), turned[:, b, :])
                        mm.then_inc(x_copied, 1)

            @blk.scalar
            def _(act):
                act.sem_inc(y_copied, 1)
                with act.Fori(0, M2 // 2) as i:
                    for u in range(2):
                        ky = i * 2 + u
                        act.wait_ge(mixed, ky + 3)
                        act.wait_ge(y_out[u], i * 16 + 16)
                        for side in range(2):
                            for b, k in ((0, 8), (1, 4)):
                                mm = act.activation(yo[:, u, 8 * b:8 * b + k, side, :],
                                                    prod[side][:, b, 0:64 * k].rearrange("p (k n) -> p k n", n=64), ACT.Copy)
                        mm.then_inc(y_copied, 1)
                        act.wait_ge(y_copied, ky + 2)
                        act.dma_start(T["Yk"][ky], yo[:, u, :, :, :].rearrange("p k s n -> p (k s n)").rearrange("p (r c) -> p r c", c=C)).then_inc(y_out[u], 16)
                for u in range(2):
                    act.wait_ge(y_out[u], 16 * (M2 // 2 + 1))

            @blk.tensor
            def _(pe):
                pe.sem_inc(x_turned, 2)
                pe.sem_inc(mixed, 2)
                pe.sem_inc(y_out[0], 16)
                pe.sem_inc(y_out[1], 16)
                pe.sem_inc(x_copied, 1)
                pe.wait_ge(consts_in, 16 * 9)
                with pe.Fori(0, M2 // 2) as i:
                    for u in range(2):
                        ky = i * 2 + u
                        pe.wait_ge(x_in[u], i * 16 + 16)
                        pe.wait_ge(x_copied, ky + 1)
                        for k in range(M1):
                            mm = pe.transpose(turned[:, k // 4, 128 * (k % 4):128 * (k % 4) + 128], xi[:, u, k, :], ident[:, :])
                        mm.then_inc(x_turned, 1)
                        pe.wait_ge(x_copied, ky + 2)
                        pe.wait_ge(w_cut, ky + 1)
                        pe.wait_ge(y_copied, ky + 1)
                        for k in range(M1):
                            for side in range(2):
                                p = 64 * side
                                mm = pe.matmul(prod[side][:, k // 8, 64 * (k % 8):64 * (k % 8) + 64], xt[p:p + 64, k, :],
                                               wk[p:p + 64, u, k, :, :].rearrange("p r c -> p (r c)"), start=True, stop=True)
                        mm.then_inc(mixed, 1)


def layer_norm_rows(dve, pool, m, src, dst, sums, tmp, step, rooted, consts, base=0):
    n, w = src.shape[1], src.shape[2]
    wide = lambda v: v.unsqueeze(2).broadcast_to([128, n, w])
    if pool is not None:
        pool.wait_ge(step, base + 6)
        pool.tensor_tensor(sums[:, 2, :], sums[:, 1, :], consts[:, 0, :], ALU.pow).then_inc(rooted, 1)
        return
    ops = [lambda: dve.tensor_reduce(sums[:, 0, :], src, AX.X, ALU.add),
           lambda: dve.tensor_scalar(sums[:, 0, :], sums[:, 0, :], 1.0 / w, None, ALU.mult),
           lambda: dve.tensor_tensor(dst, src, wide(sums[:, 0, :]), ALU.subtract),
           lambda: dve.tensor_tensor(tmp, dst, dst, ALU.mult),
           lambda: dve.tensor_reduce(sums[:, 1, :], tmp, AX.X, ALU.add),
           lambda: dve.tensor_scalar(sums[:, 1, :], sums[:, 1, :], 1.0 / w, EPS, ALU.mult, ALU.add)]
    for k, op in enumerate(ops):
        if base + k:
            dve.wait_ge(step, base + k)
        op().then_inc(step, 1)
    dve.wait_ge(rooted, 1)
    dve.tensor_tensor(dst, dst, wide(sums[:, 2, :]), ALU.mult).then_inc(step, 1)
    return base + 7


def attention_pass(nc, T):
    KT, QB = H, IMAGES * H // 512
    with ExitStack() as ctx:
        m = Store(nc, ctx, "at")
        ident = m.sb("ident", [128, 128])
        y = m.sb("y", [128, H, W])
        f2 = m.sb("f2", [128, H, 2, W], F32R)
        ft = m.sb("ft", [128, H, 128], F32R)
        fts = m.sb("fts", [128, H, 128], F32R)
        sums = m.sb("sums", [128, 6, H])
        consts = m.sb("consts", [128, 2, H])
        qs = m.sb("qs", [128, 2, 512], F32R)
        p = m.sb("p", [128, 4, 1024])
        tmp = p[:, :, :].rearrange("p a (b w) -> p (a b) w", w=W)
        p_hi = m.sb("p_hi", [128, 4, 1024], F32R)
        p_lo = m.sb("p_lo", [128, 4, 1024], F32R)
        dens = m.sb("dens", [128, H, QB])
        ot = m.sb("ot", [128, 2, 512])
        score = [m.ps(f"score{k}", [128, 2, 512]) for k in range(2)]
        acc = [m.ps(f"acc{k}", [128, 512]) for k in range(2)]
        back = m.ps("back", [128, 512])
        o = y
        den = m.sb("den", [128, H])

        loaded_in, zeroed, step, rooted = m.sem("loaded_in"), m.sem("zeroed"), m.sem("step"), m.sem("rooted")
        turned, turn_copied = m.sem("turned"), m.sem("turn_copied")
        q_copied, scored, exped, summed = m.sem("q_copied"), m.sem("scored"), m.sem("exped"), m.sem("summed")
        hi_even, hi_odd, lo_made = m.sem("hi_even"), m.sem("hi_odd"), m.sem("lo_made")
        acc_copied, o_turned, o_copied, stored_out = m.sem("acc_copied"), m.sem("o_turned"), m.sem("o_copied"), m.sem("stored_out")
        NP = KT // 2
        PRE = 14
        FINAL = PRE + 12

        def blocks(eng, body):
            for b in range(2):
                body(b, b)
            with eng.Fori(1, QB // 2 - 1) as i:
                for u in range(2):
                    body(i * 2 + u, u)
            for b in range(QB - 2, QB):
                body(b, b % 2)

        is_last = lambda b: isinstance(b, int) and b == QB - 1
        is_first = lambda b: isinstance(b, int) and b == 0

        def split_hi(eng, copy, b, k, made):
            n = b * NP + k
            wait(eng, exped, n * 2 + 2)
            wait(eng, summed, n - 3)
            copy(p_hi[:, k % 4, :], p[:, k % 4, :]).then_inc(made, 1)

        with nc.Block() as blk:
            @blk.sync
            def _(sp):
                sp.dma_start(y[:, :, :], T["tok_rows"]).then_inc(loaded_in, 16)
                sp.dma_start(ident[:, :], T["k_ident"]).then_inc(loaded_in, 16)
                sp.wait_ge(step, PRE + 8)
                sp.dma_start(tmp, T["tok_rows"]).then_inc(loaded_in, 16)
                sp.wait_ge(step, FINAL)
                sp.dma_start(T["att_rows"], tmp).then_inc(stored_out, 16)
                sp.wait_ge(stored_out, 16)

            @blk.gpsimd
            def _(pool):
                pool.memset(consts[:, 0, :], -0.5).then_inc(zeroed, 1)
                pool.wait_ge(zeroed, 1)
                pool.memset(consts[:, 1, :], 0.5).then_inc(zeroed, 1)
                pool.wait_ge(zeroed, 2)
                layer_norm_rows(None, pool, m, y[:, :, :], y, sums, tmp, step, rooted, consts)
                pool.wait_ge(step, 9)
                pool.tensor_tensor(sums[:, 4, :], sums[:, 3, :], consts[:, 1, :], ALU.pow).then_inc(rooted, 1)
                pool.wait_ge(step, PRE + 8)
                pool.tensor_tensor(sums[:, 4, :], sums[:, 3, :], consts[:, 1, :], ALU.pow).then_inc(rooted, 1)

            @blk.vector
            def _(dve):
                wide = lambda v: v.unsqueeze(2).broadcast_to([128, H, W])
                taken = [0]

                def then(ins, wait_next=True):
                    taken[0] += 1
                    ins.then_inc(step, 1)
                    if wait_next:
                        dve.wait_ge(step, taken[0])

                dve.wait_ge(loaded_in, 32)
                dve.wait_ge(zeroed, 2)
                taken[0] = layer_norm_rows(dve, None, m, y[:, :, :], y[:, :, :], sums, tmp, step, rooted, consts)
                dve.wait_ge(step, taken[0])

                def lengths(src):
                    then(dve.tensor_tensor(tmp, src, src, ALU.mult))
                    then(dve.tensor_reduce(sums[:, 3, :], tmp, AX.X, ALU.add))

                def inverse(n):
                    dve.wait_ge(rooted, n)
                    then(dve.tensor_scalar(sums[:, 4, :], sums[:, 4, :], 1e-12, None, ALU.max))
                    then(dve.reciprocal(sums[:, 5, :], sums[:, 4, :]))

                lengths(y[:, :, :])
                inverse(2)
                then(dve.tensor_tensor(y[:, :, :], y[:, :, :], wide(sums[:, 5, :]), ALU.mult))
                then(dve.tensor_copy(f2[:, :, 0, :], y[:, :, :]))
                then(dve.tensor_tensor(f2[:, :, 1, :], y[:, :, :], f2[:, :, 0, :].bitcast(F32), ALU.subtract))
                for b in range(H // 4):
                    dve.wait_ge(turned, b + 1)
                    turn = score[b % 2][:, 0, :]
                    out = [v[:, 4 * b:4 * b + 4, :].rearrange("p t n -> p (t n)") for v in (ft, fts)]
                    dve.tensor_copy(out[0], turn).then_inc(turn_copied, 1)
                    dve.tensor_copy(out[1][0:W, :], turn[W:2 * W, :]).then_inc(turn_copied, 1)
                    dve.tensor_copy(out[1][W:2 * W, :], turn[0:W, :]).then_inc(turn_copied, 1)
                dve.wait_ge(turn_copied, 3 * H // 4)

                def cut(b, u):
                    dve.tensor_copy(qs[:, u, :], ft[:, :, :].rearrange("p t n -> p (t n)")[:, bass.ds(b * 512, 512)]).then_inc(q_copied, 1)

                def put_back(b):
                    wait(dve, o_turned, b + 1)
                    src = back[:, :].rearrange("p (t a w) -> p t a w", a=2, w=W)
                    dve.tensor_copy(o[:, bass.ds(b * 4, 4), :], src[:, :, 0, :]).then_inc(o_copied, 1)
                    dve.wait_ge(o_copied, b * 2 + 1)
                    dve.tensor_tensor(o[:, bass.ds(b * 4, 4), :], o[:, bass.ds(b * 4, 4), :], src[:, :, 1, :], ALU.add).then_inc(o_copied, 1)

                def acc_out(b, u):
                    wait(dve, summed, b * NP + NP)
                    wait(dve, o_turned, b - 1)
                    dve.tensor_copy(ot[:, u, :], acc[u][:, :]).then_inc(acc_copied, 1)

                def split_lo(b, k):
                    n = b * NP + k
                    wait(dve, hi_odd if k % 2 else hi_even, b * (NP // 2) + k // 2 + 1)
                    dve.tensor_tensor(p_lo[:, k % 4, :], p[:, k % 4, :], p_hi[:, k % 4, :].bitcast(F32), ALU.subtract).then_inc(lo_made, 1)

                def body(b, u):
                    for k in range(NP):
                        if k % 2:
                            split_hi(dve, dve.tensor_copy, b, k, hi_odd)
                        split_lo(b, k)
                        if k == 4 and not is_first(b):
                            acc_out(b - 1, 1 - u)
                        if k == 10 and not is_first(b):
                            put_back(b - 1)
                        if k == 14 and not is_last(b):
                            cut(b + 1, 1 - u)

                cut(0, 0)
                blocks(dve, body)
                acc_out(QB - 1, 1)
                put_back(QB - 1)
                dve.wait_ge(o_copied, 2 * QB)
                dve.wait_ge(exped, 2 * QB * NP)
                then(dve.tensor_reduce(sums[:, 1, :], dens[:, :, :], AX.X, ALU.add))
                then(dve.reciprocal(sums[:, 0, :], sums[:, 1, :]))
                then(dve.tensor_scalar(sums[:, 1, :], sums[:, 0, :], 0.2, None, ALU.mult))
                then(dve.tensor_tensor(o[:, :, :], o[:, :, :], wide(sums[:, 1, :]), ALU.mult))
                for part in range(2):
                    then(dve.scalar_tensor_tensor(out=o[:, :, :], in0=f2[:, :, part, :].bitcast(F32), scalar=0.8, in1=o[:, :, :],
                                                  op0=ALU.mult, op1=ALU.add))
                lengths(o[:, :, :])
                inverse(3)
                then(dve.tensor_tensor(o[:, :, :], o[:, :, :], wide(sums[:, 5, :]), ALU.mult))
                dve.wait_ge(loaded_in, 48)
                then(dve.tensor_tensor(tmp, tmp, o[:, :, :], ALU.add))

            @blk.scalar
            def _(act):
                def body(b, u):
                    for k in range(NP):
                        n = b * NP + k
                        wait(act, scored, n + 1)
                        wait(act, lo_made, n - 3)
                        for e in range(2):
                            t = 2 * k + e
                            act.activation(p[:, k % 4, 512 * e:512 * e + 512], score[k % 2][:, e, :], ACT.Exp,
                                           accum_out=dens[:, t, bass.ds(b, 1)]).then_inc(exped, 1)
                        if k % 2 == 0:
                            split_hi(act, lambda dst, src: act.activation(dst, src, ACT.Copy), b, k, hi_even)

                blocks(act, body)

            @blk.tensor
            def _(pe):
                pe.wait_ge(loaded_in, 32)
                pe.wait_ge(step, PRE)
                for b in range(H // 4):
                    if b >= 2:
                        pe.wait_ge(turn_copied, 3 * b - 3)
                    for d in range(4):
                        mm = pe.transpose(score[b % 2][:, 0, 128 * d:128 * d + 128],
                                          f2[:, 4 * b + d, :, :].rearrange("p c w -> p (c w)").bitcast(F32), ident[:, :])
                    mm.then_inc(turned, 1)
                pe.wait_ge(turn_copied, 3 * H // 4)

                def scores(b, u, k):
                    n = b * NP + k
                    if k == 0:
                        wait(pe, q_copied, b + 1)
                    wait(pe, exped, n * 2 - 2)
                    for e in range(2):
                        for keys in (ft, fts):
                            mm = pe.matmul(score[k % 2][:, e, :], keys[:, 2 * k + e, :], qs[:, u, :], start=(keys is ft), stop=(keys is fts))
                    mm.then_inc(scored, 1)

                def weighted(b, u, k):
                    n = b * NP + k
                    wait(pe, lo_made, n + 1)
                    if k == 0:
                        wait(pe, acc_copied, b - 1)
                    for e in range(2):
                        t = 2 * k + e
                        for part in (p_hi, p_lo):
                            mm = pe.matmul(acc[u][:, :], f2[:, t, :, :].rearrange("p c w -> p (c w)"), part[:, k % 4, 512 * e:512 * e + 512],
                                           start=(t == 0 and part is p_hi), stop=(t == KT - 1 and part is p_lo))
                    mm.then_inc(summed, 1)

                def turn_back(b, u):
                    wait(pe, acc_copied, b + 1)
                    wait(pe, o_copied, b * 2)
                    for d in range(4):
                        mm = pe.transpose(back[:, 128 * d:128 * d + 128], ot[:, u, 128 * d:128 * d + 128], ident[:, :])
                    mm.then_inc(o_turned, 1)

                LAG = 3

                def body(b, u):
                    for k in range(NP):
                        scores(b, u, k)
                        if k >= LAG:
                            weighted(b, u, k - LAG)
                        elif not is_first(b):
                            weighted(b - 1, 1 - u, NP + k - LAG)
                        if k == 10 and not is_first(b):
                            turn_back(b - 1, 1 - u)

                blocks(pe, body)
                for k in range(NP - LAG, NP):
                    weighted(QB - 1, 1, k)
                turn_back(QB - 1, 1)


HEADS, DIM, NKEYS, TOPK = 8, 64, 64, 16
NKV = NKEYS * NKEYS
KCH = NKV // 128
TT = IMAGES * H // 128
LOWEST = -3.0e38


def ffn_prepare(nc, T):
    with ExitStack() as ctx:
        m = Store(nc, ctx, "fp")
        ident = m.sb("ident", [128, 128])
        h = m.sb("h", [128, TT, W])
        y = m.sb("y", [128, TT, W])
        tmp = m.sb("tmp", [128, TT, W])
        xt = m.sb("xt", [W, TT, 128])
        sums = m.sb("sums", [128, 3, TT])
        consts = m.sb("consts", [128, 1, TT])
        wq = m.sb("wq", [DIM, 4, 128])
        keys = m.sb("keys", [NKEYS, 4, 128])
        wqt = m.sb("wqt", [128, 4, DIM])
        keyst = m.sb("keyst", [128, 4, NKEYS])
        both = m.sb("both", [DIM, HEADS, 2, NKEYS])
        bank = [m.ps(f"bank{k}", [128, 512]) for k in range(2)]
        wbank = [m.ps(f"wbank{k}", [128, 512]) for k in range(4)]
        loaded_in, zeroed, step, rooted = m.sem("loaded_in"), m.sem("zeroed"), m.sem("step"), m.sem("rooted")
        turned, copied = m.sem("turned"), m.sem("copied")
        w_turned, w_copied, w_made, both_copied, stored_out = (m.sem("w_turned"), m.sem("w_copied"), m.sem("w_made"),
                                                               m.sem("both_copied"), m.sem("stored_out"))
        with nc.Block() as blk:
            @blk.sync
            def _(sp):
                sp.dma_start(h[:, :, :], T["att_tiles"]).then_inc(loaded_in, 16)
                sp.dma_start(ident[:, :], T["k_ident"]).then_inc(loaded_in, 16)
                sp.dma_start(wq[:, :, :].rearrange("p a b -> p (a b)"), T["Wq_pk"]).then_inc(loaded_in, 16)
                for p in range(2):
                    sp.dma_start(keys[:, 2 * p:2 * p + 2, :].rearrange("k a b -> k (a b)"),
                                 T["pk_keys"][p].rearrange("k h d -> k (h d)")).then_inc(loaded_in, 16)
                sp.wait_ge(both_copied, 4)
                sp.dma_start(T["both"], both[:, :, :, :].rearrange("d h p k -> d h (p k)")).then_inc(stored_out, 16)
                sp.wait_ge(copied, TT // 4)
                sp.dma_start(T["xt"], xt[:, :, :]).then_inc(stored_out, 16)
                sp.wait_ge(stored_out, 32)

            @blk.gpsimd
            def _(pool):
                pool.memset(consts[:, 0, :], -0.5).then_inc(zeroed, 1)
                pool.wait_ge(zeroed, 1)
                layer_norm_rows(None, pool, m, y[:, :, :], y, sums, tmp, step, rooted, consts)

            @blk.vector
            def _(dve):
                dve.wait_ge(loaded_in, 16 * 5)
                dve.wait_ge(w_turned, 1)
                dve.tensor_copy(wqt[:, :, :].rearrange("p c d -> p (c d)"), wbank[0][:, 0:256]).then_inc(w_copied, 1)
                dve.wait_ge(w_turned, 2)
                dve.tensor_copy(keyst[:, :, :].rearrange("p c k -> p (c k)"), wbank[1][:, 0:256]).then_inc(w_copied, 1)
                dve.wait_ge(w_made, 1)
                for hh in range(4):
                    dve.tensor_copy(both[:, hh::4, :, :].rearrange("d a p k -> d p a k"),
                                    wbank[hh][0:DIM, 0:256].rearrange("d (p a k) -> d p a k", p=2, a=2)).then_inc(both_copied, 1)
                layer_norm_rows(dve, None, m, h[:, :, :], y[:, :, :], sums, tmp[:, :, :], step, rooted, consts)
                for b in range(TT // 4):
                    dve.wait_ge(turned, b + 1)
                    dve.tensor_copy(xt[:, 4 * b:4 * b + 4, :].rearrange("p t n -> p (t n)"), bank[b % 2][0:W, :]).then_inc(copied, 1)

            @blk.tensor
            def _(pe):
                pe.wait_ge(loaded_in, 16 * 5)
                for src, dst in ((wq, wbank[0]), (keys, wbank[1])):
                    for c in range(4):
                        mm = pe.transpose(dst[:, 64 * c:64 * c + 64], src[:, c, :], ident[0:64, 0:64])
                    mm.then_inc(w_turned, 1)
                pe.wait_ge(w_copied, 2)
                for c in range(4):
                    for hh in range(4):
                        rows = slice(32 * hh, 32 * hh + 32)
                        mm = pe.matmul(wbank[hh][0:DIM, 64 * c:64 * c + 64], wqt[rows, c, :], keyst[rows, c, :], start=True, stop=True)
                mm.then_inc(w_made, 1)
                pe.wait_ge(step, 7)
                for b in range(TT // 4):
                    if b >= 2:
                        pe.wait_ge(copied, b - 1)
                    for d in range(4):
                        mm = pe.transpose(bank[b % 2][0:W, 128 * d:128 * d + 128], y[:, 4 * b + d, :], ident[:, :])
                    mm.then_inc(turned, 1)


class Tile:

    def __init__(self, head, quarter, lane, fixed):
        self.head, self.quarter, self.lane, self.fixed = head, quarter, lane, fixed

    @property
    def index(self):
        return self.quarter * 4 + self.lane

    @property
    def n(self):
        return self.head * TT + self.quarter * 4 + self.lane

    @property
    def half_uses(self):
        return self.head * (TT // 2) + self.quarter * 2 + (self.lane // 2 + 1)

    @property
    def slot(self):
        return self.lane % 2

    @property
    def exists(self):
        return not self.fixed or 0 <= self.index < TT

    def back(self, d):
        carry, lane = divmod(self.lane - d, 4)
        return Tile(self.head, self.quarter + carry, lane, self.fixed)


def tile_times(eng, head, body, extra=3):
    for t in range(4):
        body(Tile(head, 0, t, True))
    with eng.Fori(1, TT // 4 - 1) as quarter:
        for lane in range(4):
            body(Tile(head, quarter, lane, False))
    for t in range(TT - 4, TT + extra):
        body(Tile(head, t // 4, t % 4, True))


START = 64


def wait_n(eng, sem, value):
    eng.wait_ge(sem, value + START)


def own_step(eng, sem, value):
    eng.wait_ge(sem, value + START)
    eng.nop(nofuse=True)


def ffn_pass(nc, T):
    with ExitStack() as ctx:
        m = Store(nc, ctx, "ff")
        ident = m.sb("ident", [128, 128])
        causal = m.sb("causal", [128, 128])
        out = m.sb("out", [128, TT, W])
        table = m.sb("table", [128, 2, KCH, 2 * DIM])
        both = m.sb("both", [DIM, 2, 128])
        wq = m.sb("wq", [DIM, 2, DIM])
        wo = m.sb("wo", [DIM, 2, DIM])
        x = m.sb("x", [DIM, 2, 128])
        sim = m.sb("sim", [128, 2, 128])
        q = m.sb("q", [DIM, 4, 128])
        cut = m.sb("cut", [128, 256])
        best = m.sb("best", [128, 2, TOPK])
        cand = m.sb("cand", [128, TOPK, TOPK])
        top = m.sb("top", [128, 2, TOPK])
        topexp = m.sb("topexp", [128, TOPK])
        nmax = m.sb("nmax", [128, 2, 1])
        total = m.sb("total", [128, 4, 1])
        inv = m.sb("inv", [128, 1])
        pairs = m.sb("pairs", [128, 2, NKEYS, NKEYS])
        wt = m.sb("wt", [128, 2, NKV])
        wtt = m.sb("wtt", [128, KCH, 128])
        kv = m.sb("kv", [128, 2 * DIM])
        kt = m.sb("kt", [DIM, 128])
        att = m.sb("att", [128, 128])
        amax = m.sb("amax", [128, 2])
        prob = m.sb("prob", [128, 128])
        rowsum = m.sb("rowsum", [128, 2])
        probn = m.sb("probn", [128, 128])
        probt = m.sb("probt", [128, 128])
        ot = m.sb("ot", [DIM, 128])
        simp = m.ps("simp", [128, 512])
        turnp = [m.ps(f"turnp{k}", [128, 512]) for k in range(4)]
        kvp = [m.ps(f"kvp{k}", [128, 512]) for k in range(2)]
        tailp = m.ps("tailp", [128, 512])

        consts_in = m.sem("consts_in")
        head_in = [m.sem(f"head_in{k}") for k in range(2)]
        x_in = [m.sem(f"x_in{k}") for k in range(2)]
        sim_made, sim_copied, q_copied = m.sem("sim_made"), m.sem("sim_copied"), m.sem("q_copied")
        top_step, topped, exped_top, paired = m.sem("top_step"), m.sem("topped"), m.sem("exped_top"), m.sem("paired")
        exped, masked = m.sem("exped"), m.sem("masked")
        turned, copied_a, copied_v, kv_made = m.sem("turned"), m.sem("copied_a"), m.sem("copied_v"), m.sem("kv_made")
        inverted, kv_scaled, kt_made, kt_copied = m.sem("inverted"), m.sem("kv_scaled"), m.sem("kt_made"), m.sem("kt_copied")
        att_made, att_masked, att_max, att_neg = m.sem("att_made"), m.sem("att_masked"), m.sem("att_max"), m.sem("att_neg")
        att_exp, att_inv, att_scaled = m.sem("att_exp"), m.sem("att_inv"), m.sem("att_scaled")
        probt_made, probt_copied, ot_made, ot_copied = m.sem("probt_made"), m.sem("probt_copied"), m.sem("ot_made"), m.sem("ot_copied")
        o_made, o_added, stored_out = m.sem("o_made"), m.sem("o_added"), m.sem("stored_out")
        HEAD_LOADS = 2 * KCH // 8 + 3
        UNITS = KCH // 4

        def heads(eng, body, before=None):
            with eng.Fori(0, HEADS // 2) as pair:
                for u in range(2):
                    if before:
                        before(pair, u)
                    tile_times(eng, pair * 2 + u, lambda t, u=u, pair=pair: body(t, u, pair))

        with nc.Block() as blk:
            @blk.sync
            def _(sp):
                for sem in m.sems:
                    sp.sem_inc(sem, START)

        with nc.Block() as blk:
            @blk.sync
            def _(sp):
                sp.dma_start(ident[:, :], T["k_ident"]).then_inc(consts_in, 16)
                sp.dma_start(causal[:, :], T["k_causal"]).then_inc(consts_in, 16)
                sp.dma_start(out[:, :, :], T["att_tiles"]).then_inc(consts_in, 16)

                def load_head(pair, u):
                    head = pair * 2 + u
                    wait_n(sp, o_added, (head - 1) * TT)
                    for at in range(0, KCH, 8):
                        sp.dma_start(table[:, u, at:at + 8, 0:DIM], T["keys_chunks"][head][:, at:at + 8, :]).then_inc(head_in[u], 16)
                        sp.dma_start(table[:, u, at:at + 8, DIM:2 * DIM], T["values_chunks"][head][:, at:at + 8, :]).then_inc(head_in[u], 16)
                    sp.dma_start(both[:, u, :], T["both_heads"][head]).then_inc(head_in[u], 16)
                    sp.dma_start(wq[:, u, :], T["Wq_heads"][head]).then_inc(head_in[u], 16)
                    sp.dma_start(wo[:, u, :], T["Wo_heads"][head]).then_inc(head_in[u], 16)

                def body(t, u, pair):
                    if t.exists:
                        wait_n(sp, sim_made, t.n - 1)
                        sp.dma_start(x[:, t.slot, :], T["xt_tiles"][t.index]).then_inc(x_in[t.slot], 16)
                    if u == 0 and t.fixed and isinstance(t.index, int) and t.index == 3:
                        load_head(pair, 1)

                heads(sp, body, lambda pair, u: load_head(pair, 0) if u == 0 else None)
                wait_n(sp, o_added, HEADS * TT)
                sp.dma_start(T["out_tiles"], out[:, :, :]).then_inc(stored_out, 16)
                wait_n(sp, stored_out, 16)

            @blk.gpsimd
            def _(pool):
                def body(t, u, pair):
                    if not t.exists:
                        return
                    wait_n(pool, sim_copied, t.n + 1)
                    for c in range(4):
                        wait_n(pool, masked, (t.n - 2) * 4 + c + 1)
                        pool.tensor_tensor(pairs[:, t.slot, 16 * c:16 * c + 16, :],
                                           sim[:, t.slot, 64 + 16 * c:64 + 16 * c + 16].unsqueeze(2).broadcast_to([128, 16, NKEYS]),
                                           sim[:, t.slot, 0:64].unsqueeze(1).broadcast_to([128, 16, NKEYS]), ALU.add).then_inc(paired, 1)

                heads(pool, body)

            @blk.vector
            def _(dve):
                def bests(t, part):
                    if not t.exists:
                        return
                    base = t.n * 9
                    if part < 2:
                        side = sim[:, t.slot, 64 * part:64 * part + 64]
                        if part == 0:
                            own_step(dve, sim_copied, t.n + 1)
                        dve.max(best[:, part, 0:8], side).then_inc(top_step, 1)
                        own_step(dve, top_step, base + 3 * part + 1)
                        dve.match_replace(cut[:, 0:64], best[:, part, 0:8], side, LOWEST).then_inc(top_step, 1)
                        own_step(dve, top_step, base + 3 * part + 2)
                        dve.max(best[:, part, 8:16], cut[:, 0:64]).then_inc(top_step, 1)
                    flat = cand[:, :, :].rearrange("p a b -> p (a b)")
                    if part == 2:
                        own_step(dve, top_step, base + 6)
                        dve.tensor_tensor(cand[:, :, :], best[:, 0, :].unsqueeze(2).broadcast_to([128, TOPK, TOPK]),
                                          best[:, 1, :].unsqueeze(1).broadcast_to([128, TOPK, TOPK]), ALU.add).then_inc(top_step, 1)
                        own_step(dve, top_step, base + 7)
                        own_step(dve, exped_top, t.n - 1)
                        own_step(dve, exped, (t.n - 1) * 4)
                        dve.max(top[:, t.slot, 0:8], flat).then_inc(top_step, 1)
                        own_step(dve, top_step, base + 8)
                        dve.match_replace(cut[:, :], top[:, t.slot, 0:8], flat, LOWEST).then_inc(top_step, 1)
                    if part == 3:
                        own_step(dve, top_step, base + 9)
                        dve.max(top[:, t.slot, 8:16], cut[:, :]).then_inc(topped, 1)
                        dve.tensor_scalar(nmax[:, t.slot, :], top[:, t.slot, 0:1], -1.0, None, ALU.mult).then_inc(topped, 1)

                def weights(t, c):
                    if t.exists:
                        wait_n(dve, exped, t.n * 4 + c + 1)
                        wait_n(dve, topped, t.n * 2 + 2)
                        part = wt[:, t.slot, 1024 * c:1024 * c + 1024]
                        dve.scalar_tensor_tensor(out=part, in0=pairs[:, t.slot, 16 * c:16 * c + 16, :].rearrange("p b a -> p (b a)"),
                                                 scalar=top[:, t.slot, 15:16], in1=part, op0=ALU.is_ge, op1=ALU.mult).then_inc(masked, 1)

                def copy_turned(t, k):
                    if t.exists:
                        wait_n(dve, turned, t.n * UNITS + k + 1)
                        wait_n(dve, kv_made, (t.n - 1) * UNITS + k + 1)
                        dve.tensor_copy(wtt[:, 4 * k:4 * k + 4, :].rearrange("p c n -> p (c n)"), turnp[k % 4][:, :]).then_inc(copied_v, 1)

                def scale_kv(t):
                    if t.exists:
                        wait_n(dve, exped_top, t.n + 1)
                        dve.reciprocal(inv[:, :], total[:, t.lane, :]).then_inc(inverted, 1)
                        wait_n(dve, inverted, t.n + 1)
                        wait_n(dve, kv_made, t.n * UNITS + UNITS)
                        wait_n(dve, ot_made, t.n)
                        dve.tensor_scalar(kv[:, :], kvp[t.slot][:, 0:128], inv[:, 0:1], None, ALU.mult).then_inc(kv_scaled, 1)

                def mask_att(t):
                    if t.exists:
                        wait_n(dve, att_made, t.n + 1)
                        dve.tensor_tensor(att[:, :], tailp[:, 0:128], causal[:, :], ALU.add).then_inc(att_masked, 1)
                        wait_n(dve, att_masked, t.n + 1)
                        dve.tensor_reduce(amax[:, 0:1], att[:, :], AX.X, ALU.max).then_inc(att_max, 1)
                        wait_n(dve, att_max, t.n + 1)
                        dve.tensor_scalar(amax[:, 1:2], amax[:, 0:1], -1.0, None, ALU.mult).then_inc(att_neg, 1)

                def scale_att(t):
                    if t.exists:
                        wait_n(dve, att_exp, t.n + 1)
                        dve.reciprocal(rowsum[:, 1:2], rowsum[:, 0:1]).then_inc(att_inv, 1)
                        wait_n(dve, att_inv, t.n + 1)
                        dve.tensor_scalar(probn[:, :], prob[:, :], rowsum[:, 1:2], None, ALU.mult).then_inc(att_scaled, 1)

                def copy_ot(t):
                    if t.exists:
                        wait_n(dve, ot_made, t.n + 1)
                        dve.tensor_copy(ot[:, :], tailp[0:DIM, 0:128]).then_inc(ot_copied, 1)

                def add_out(t):
                    if t.exists:
                        wait_n(dve, o_made, t.n + 1)
                        row = out[:, bass.ds(t.index, 1), :].rearrange("p o w -> p (o w)")
                        dve.tensor_tensor(row, tailp[:, 0:W], row, ALU.add).then_inc(o_added, 1)

                def body(t, u, pair):
                    scale_kv(t.back(3))
                    for k in range(UNITS):
                        if k % 2 == 1:
                            copy_turned(t.back(2), k)
                            weights(t.back(1), k // 2)
                        else:
                            bests(t, k // 2)
                        if k == 2:
                            mask_att(t.back(3))
                        if k == 4:
                            scale_att(t.back(3))
                        if k == 6:
                            copy_ot(t.back(3))
                    add_out(t.back(3))

                wait_n(dve, consts_in, 48)
                heads(dve, body)

            @blk.scalar
            def _(act):
                def copy_sim(t):
                    if t.exists:
                        wait_n(act, sim_made, t.n + 1)
                        wait_n(act, paired, (t.n - 1) * 4)
                        wait_n(act, topped, (t.n - 1) * 2)
                        wait_n(act, att_made, t.n - 3)
                        act.activation(sim[:, t.slot, :], simp[:, 0:128], ACT.Copy).then_inc(sim_copied, 1)
                        act.activation(q[:, t.lane, :], simp[0:DIM, 128:256], ACT.Copy, scale=DIM ** -0.5).then_inc(q_copied, 1)

                def exp_top(t):
                    if t.exists:
                        wait_n(act, topped, t.n * 2 + 2)
                        wait_n(act, inverted, t.n - 3)
                        wait_n(act, exped_top, t.n)
                        act.activation(topexp[:, :], top[:, t.slot, :], ACT.Exp, bias=nmax[:, t.slot, :],
                                       accum_out=total[:, t.lane, :]).then_inc(exped_top, 1)

                def exp_pairs(t, c):
                    if t.exists:
                        wait_n(act, paired, t.n * 4 + c + 1)
                        wait_n(act, turned, (t.n - 2) * UNITS + 2 * c + 2)
                        act.activation(wt[:, t.slot, 1024 * c:1024 * c + 1024],
                                       pairs[:, t.slot, 16 * c:16 * c + 16, :].rearrange("p b a -> p (b a)"),
                                       ACT.Exp, bias=nmax[:, t.slot, :]).then_inc(exped, 1)

                def copy_turned(t, k):
                    if t.exists:
                        wait_n(act, turned, t.n * UNITS + k + 1)
                        wait_n(act, kv_made, (t.n - 1) * UNITS + k + 1)
                        act.activation(wtt[:, 4 * k:4 * k + 4, :].rearrange("p c n -> p (c n)"), turnp[k % 4][:, :], ACT.Copy).then_inc(copied_a, 1)

                def copy_kt(t):
                    if t.exists:
                        wait_n(act, kt_made, t.n + 1)
                        act.activation(kt[:, :], tailp[0:DIM, 0:128], ACT.Copy).then_inc(kt_copied, 1)

                def exp_att(t):
                    if t.exists:
                        wait_n(act, att_neg, t.n + 1)
                        act.activation(prob[:, :], att[:, :], ACT.Exp, bias=amax[:, 1:2], accum_out=rowsum[:, 0:1]).then_inc(att_exp, 1)

                def copy_probt(t):
                    if t.exists:
                        wait_n(act, probt_made, t.n + 1)
                        act.activation(probt[:, :], tailp[:, 0:128], ACT.Copy).then_inc(probt_copied, 1)

                def body(t, u, pair):
                    copy_sim(t)
                    for k in range(UNITS):
                        if k == 0:
                            exp_top(t.back(1))
                        if k % 2 == 0:
                            copy_turned(t.back(2), k)
                            exp_pairs(t.back(1), k // 2)
                        if k == 1:
                            copy_kt(t.back(3))
                        if k == 3:
                            exp_att(t.back(3))
                        if k == 5:
                            copy_probt(t.back(3))

                heads(act, body)

            @blk.tensor
            def _(pe):
                def sims(t, u, pair):
                    if not t.exists:
                        return
                    wait_n(pe, x_in[t.slot], t.half_uses * 16)
                    wait_n(pe, q_copied, t.n)
                    if t.fixed and t.index == 0:
                        wait_n(pe, head_in[u], (pair + 1) * (16 * HEAD_LOADS))
                    pe.matmul(simp[:, 0:128], x[:, t.slot, :], both[:, u, :], start=True, stop=True)
                    pe.matmul(simp[0:DIM, 128:256], wq[:, u, :], x[:, t.slot, :], start=True, stop=True).then_inc(sim_made, 1)

                def turn(t, k):
                    if not t.exists:
                        return
                    wait_n(pe, masked, t.n * 4 + k // 2 + 1)
                    wait_n(pe, (copied_a, copied_v)[k % 2], t.n * 4 + k // 2 - 1)
                    for d in range(4):
                        at = 128 * (4 * k + d)
                        mm = pe.transpose(turnp[k % 4][:, 128 * d:128 * d + 128], wt[:, t.slot, at:at + 128], ident[:, :])
                    mm.then_inc(turned, 1)

                def lookup(t, u, k):
                    if not t.exists:
                        return
                    if k == 0:
                        wait_n(pe, kv_scaled, t.n - 1)
                    wait_n(pe, (copied_a, copied_v)[k % 2], t.n * 4 + k // 2 + 1)
                    for c in range(4 * k, 4 * k + 4):
                        mm = pe.matmul(kvp[t.slot][:, 0:128], wtt[:, c, :], table[:, u, c, :], start=(c == 0), stop=(c == KCH - 1))
                    mm.then_inc(kv_made, 1)

                def tail(t, u, step):
                    if not t.exists:
                        return
                    if step == 0:
                        wait_n(pe, kv_scaled, t.n + 1)
                        wait_n(pe, o_added, t.n)
                        pe.transpose(tailp[:, 0:128], kv[:, :], ident[:, :]).then_inc(kt_made, 1)
                    if step == 1:
                        wait_n(pe, kt_copied, t.n + 1)
                        pe.matmul(tailp[:, 0:128], q[:, t.lane, :], kt[:, :], start=True, stop=True).then_inc(att_made, 1)
                    if step == 2:
                        wait_n(pe, att_scaled, t.n + 1)
                        pe.transpose(tailp[:, 0:128], probn[:, :], ident[:, :]).then_inc(probt_made, 1)
                    if step == 3:
                        wait_n(pe, probt_copied, t.n + 1)
                        pe.matmul(tailp[0:DIM, 0:128], kv[:, DIM:2 * DIM], probt[:, :], start=True, stop=True).then_inc(ot_made, 1)
                    if step == 4:
                        wait_n(pe, ot_copied, t.n + 1)
                        pe.matmul(tailp[:, 0:W], ot[:, :], wo[:, u, :], start=True, stop=True).then_inc(o_made, 1)

                def body(t, u, pair):
                    sims(t, u, pair)
                    for k in range(UNITS):
                        turn(t.back(2), k)
                        if k >= 1:
                            lookup(t.back(2), u, k - 1)
                        if k in (1, 2, 5, 6, 7):
                            tail(t.back(3), u, (1, 2, 5, 6, 7).index(k))
                    lookup(t.back(2), u, UNITS - 1)

                wait_n(pe, consts_in, 48)
                heads(pe, body)


def ffn_views(nc, T):
    both = nc.dram_tensor("both", [DIM, HEADS, 128], F32, kind="Internal").ap()
    xt = nc.dram_tensor("xt", [W, TT, 128], F32, kind="Internal").ap()
    tiles = lambda v: v.rearrange("(t i) h w -> (i h) t w", i=2)
    T["both"], T["both_heads"] = both, both.rearrange("d h k -> h d k")
    T["xt"], T["xt_tiles"] = xt, xt.rearrange("w t n -> t w n")
    T["att_tiles"], T["out_tiles"] = tiles(T["att_rows"]), tiles(T["out_rows"])
    T["keys_chunks"] = T["keys_table"].rearrange("(h c p) d -> h p c d", h=HEADS, p=128)
    T["values_chunks"] = T["values_table"].rearrange("(h c p) d -> h p c d", h=HEADS, p=128)
    T["Wq_heads"] = T["Wq"].rearrange("d (h e) -> h d e", h=HEADS)
    T["Wo_heads"] = T["Wo"].rearrange("(h d) e -> h d e", h=HEADS)


def build(nc, args, out):
    T = dict(args)
    dram = lambda name, shape: nc.dram_tensor(name, shape, F32, kind="Internal").ap()
    T["h"] = [dram("h_even", [QUADS, 128, PX]), dram("h_odd", [QUADS, 128, PX])]
    for name, t in (("X", dram("spectrum_in", [M2, ROWS, IMAGES, C])), ("Y", dram("spectrum_out", [M2, ROWS, IMAGES, C]))):
        T[name] = t.rearrange("k r (q i) c -> q r k (i c)", i=QI)
        T[name + "k"] = t.rearrange("k r n c -> k n r c")
    T["x"] = T["x"].rearrange("(q i) (j r) w c -> q (i j) (r w c)", i=QI, r=2)
    T["tok_rows"] = dram("tok", [IMAGES, H, W])
    T["tok"] = T["tok_rows"].rearrange("(q i) (j r) w -> q (i j) (r w)", i=QI, r=2)
    T["att_rows"] = dram("att", [IMAGES, H, W])
    T["out_rows"] = out
    ffn_views(nc, T)
    tower_pass(nc, -1, T)
    for layer in range(LAYERS):
        mix_pass(nc, layer, T)
        tower_pass(nc, layer, T)
    attention_pass(nc, T)
    ffn_prepare(nc, T)
    ffn_pass(nc, T)


_TOK = ["fc0_w", "fc0_b", "ln0_g", "ln0_b", "w1r", "w1i", "w2r", "w2i", "conv_w", "conv_b", "ln_g", "ln_b",
        "fc1_w", "fc1_b", "fc2_w", "fc2_b", "fc3_w", "fc3_b"]
_FFN = ["Wq_pk", "pk_keys", "Wq", "keys_table", "values_table", "Wo"]


def kernel(**inputs):
    import concourse.bacc as bacc
    from concourse.bass_utils import run_bass_kernel_spmd

    nc = bacc.Bacc("TRN2", target_bir_lowering=False, num_devices=1)
    named = {"x": inputs["x"]}
    named.update({n: inputs["L0_tok_" + n] for n in _TOK})
    named.update({n: inputs["L0_ffn_" + n] for n in _FFN})
    named.update(shape_constants())
    arrays, args = {}, {}
    for name, a in named.items():
        a = np.ascontiguousarray(a)
        arrays[name + "_dram"] = a
        args[name] = nc.dram_tensor(name + "_dram", a.shape, mybir.dt.from_np(a.dtype), kind="ExternalInput").ap()
    out = nc.dram_tensor("out_dram", (IMAGES, H, W), F32, kind="ExternalOutput").ap()
    build(nc, args, out)
    r = run_bass_kernel_spmd(nc, [arrays], core_ids=[0])
    return r.results[0]["out_dram"]
```

```python
from contextlib import ExitStack

import numpy as np

import concourse.bass as bass
from concourse import mybir

F32 = mybir.dt.float32
I32 = mybir.dt.int32
F32R = mybir.dt.float32r
ACT = mybir.ActivationFunctionType
ALU = mybir.AluOpType
AX = mybir.AxisListType

IMAGES, H, W = 128, 64, 64
C, LAYERS, M1, M2 = 32, 4, 12, 12
QI = 4
QUADS = IMAGES // QI
PX = H * W
TILES = PX // 128
GROUPS = TILES // 4
ROWS = 2 * 2 * M1
EPS = 1e-5
ROOT_GUESS = 1597463007.0
ROOT_STEPS = 11


def shape_constants():
    r2, w = np.arange(2), np.arange(W)
    ky, h = np.arange(M2), np.arange(H)
    phi = 2 * np.pi * np.outer(w, ky) / W
    f1 = np.zeros((2, W, 2, M2, 2))
    for r in r2:
        f1[r, :, r, :, 0] = np.cos(phi)
        f1[r, :, r, :, 1] = -np.sin(phi)
    freq = np.stack([np.arange(M1), np.arange(H - M1, H)], 1)
    th = 2 * np.pi * h[:, None, None] * freq[None] / H
    g = np.zeros((H, 2, M1, 2, 2))
    g[:, 0, :, :, 0] = np.cos(th)
    g[:, 1, :, :, 0] = np.sin(th)
    g[:, 0, :, :, 1] = -np.sin(th)
    g[:, 1, :, :, 1] = np.cos(th)
    gi = np.zeros((M1, 2, 2, H, 2))
    tt = th.transpose(1, 2, 0)
    gi[:, :, 0, :, 0] = np.cos(tt)
    gi[:, :, 1, :, 0] = -np.sin(tt)
    gi[:, :, 0, :, 1] = np.sin(tt)
    gi[:, :, 1, :, 1] = np.cos(tt)
    weight = np.where(ky == 0, 1.0, 2.0)[:, None] / (H * W)
    e = np.zeros((97, 2, 2, W))
    ev = e[:96].reshape(4, M2, 2, 2, 2, W)
    for par in range(2):
        for r in r2:
            ev[2 * par + r, :, 0, par, r] = weight * np.cos(phi.T)
            ev[2 * par + r, :, 1, par, r] = -weight * np.sin(phi.T)
    e[96] = 1.0
    centre = np.kron(np.eye(4), np.eye(C) - 1.0 / C)
    block = np.kron(np.eye(4), np.ones((C, C)))
    fc0 = np.zeros((97, 2, 4, 4))
    fv = fc0[:96].reshape(8, 4, 3, 2, 4, 4)
    for j in range(8):
        for i in range(4):
            fv[j, i, :, j % 2, j // 2, i] = 1.0
    fc0[96] = 1.0
    pos = np.arange(128)
    causal = np.where((pos[:, None] // 64 == pos[None] // 64) & (pos[None] <= pos[:, None]), 0.0, -1e30)
    pick = np.zeros((2, 2, 32, 8, 4, 32))
    for k in range(32):
        pick[:, 0, k, :, :, k] = 1.0
        pick[:, 1, k, k // 4, k % 4, :] = 1.0
    f = lambda a, n: np.ascontiguousarray(a.reshape(n, -1), dtype=np.float32)
    return {"k_f1": f(f1, 128), "k_g": f(g, 128), "k_gi": f(gi, ROWS), "k_e": f(e, 97), "k_ident": f(np.eye(128), 128),
            "k_centre": f(centre, 128), "k_block": f(block, 128), "k_fc0": f(fc0, 97), "k_causal": f(causal, 128),
            "k_pick": f(pick, 128)}


class Quad:

    def __init__(self, half, parity, fixed):
        self.half, self.parity, self.fixed = half, parity, fixed

    @property
    def n(self):
        return self.half * 2 + self.parity

    def __add__(self, d):
        carry, parity = divmod(self.parity + d, 2)
        return Quad(self.half + carry, parity, self.fixed)

    def uses(self, before):
        return self.half + (1 - before // 2)

    @property
    def exists(self):
        return not self.fixed or 0 <= self.n < QUADS

    def back(self, slot, lag, period=GROUPS):
        d, unit = divmod(slot - lag, period)
        return self + d, unit


def quad_times(eng, body, first=-1, last=QUADS + 2):
    for n in range(first, 2):
        body(Quad(n // 2, n % 2, True))
    with eng.Fori(1, QUADS // 2 - 1) as pair:
        for u in range(2):
            body(Quad(pair, u, False))
    for n in range(QUADS - 2, last):
        body(Quad(n // 2, n % 2, True))


def forward_units(q, s):
    early, middle, late = {5: 4, 6: 7}, {5: 5, 6: 8}, {0: 1, 2: 2, 4: 3, 5: 6, 6: 9}
    places = [[(q + -1, units[s])] if s in units else [] for units in (early, middle, late)]
    if s == 7:
        places[0].append((q, 0))
    return places


def wait(eng, sem, value):
    if not isinstance(value, int) or value > 0:
        eng.wait_ge(sem, value)


def tile_of(g, t):
    return 8 * (g // 2) + 2 * t + g % 2


class Store:

    def __init__(self, nc, ctx, prefix):
        self.nc, self.ctx, self.prefix = nc, ctx, prefix
        self.sems = []
        ctx.callback(self.release)

    def release(self):
        self.nc.clear_and_free_semaphores(self.sems)
        self.nc.all_engine_barrier()

    def sb(self, name, shape, dtype=F32):
        return self.ctx.enter_context(self.nc.sbuf_tensor(f"{self.prefix}_{name}", shape, dtype))

    def ps(self, name, shape):
        return self.ctx.enter_context(self.nc.psum_tensor(f"{self.prefix}_{name}", shape, F32))

    def sem(self, name):
        self.sems.append(self.nc.alloc_semaphore(f"{self.prefix}_{name}"))
        return self.sems[-1]


def tower_pass(nc, layer, T):
    first, final = layer < 0, layer == LAYERS - 1
    fwd = not final
    ZU = 2 if first else 7
    FU = 10
    with ExitStack() as ctx:
        m = Store(nc, ctx, f"p{layer + 1}")
        ident = m.sb("ident", [128, 128])
        gain = m.sb("gain", [128, 1])
        shift = m.sb("shift", [128, 1])
        BATCH = 1 if final else 2
        ssq = m.sb("ssq", [128, 2, BATCH * 16])
        rstd = m.sb("rstd", [128, 2, BATCH * 16])
        newton = m.sb("newton", [128, BATCH * 16])
        square = m.sb("square", [128, 2, 512])
        normed = m.sb("normed", [128, 2, 512])
        if first:
            xs = m.sb("xs", [128, 2, 128, 3])
            xb = m.sb("xb", [128, TILES, QI, 3])
            xt = m.sb("xt", [97, 2, 4, 128])
            fc0 = m.sb("fc0", [97, 32, C])
            mask = m.sb("mask", [97, 32])
            fc0w = m.sb("fc0w", [97, C])
            fc0sum = m.sb("fc0sum", [97, 1])
            fc0mean = m.sb("fc0mean", [97, 1])
            fc0c = m.sb("fc0c", [97, C])
        else:
            hin = m.sb("hin", [128, 2, PX])
            yq = m.sb("yq", [ROWS, 2, M2, 128])
            z1 = m.sb("z1", [128, H, M2, 2])
            z2 = m.sb("z2", [97, 2, 16, 128])
            gi = m.sb("gi", [ROWS, 128])
            emat = m.sb("emat", [97, 2, 128])
            centre = m.sb("centre", [128, 128])
            block = m.sb("block", [128, 4, C])
            convrow = m.sb("convrow", [128, C])
            convdiag = m.sb("convdiag", [128, 4, C])
            wconv = m.sb("wconv", [128, 128])
            biascol = m.sb("biascol", [128, 97])
        NACC = 2 if final else 4
        accs = [m.ps(f"acc{k}", [128, 512]) for k in range(NACC)]
        ta = m.ps("ta", [128, 512])
        zbank = m.ps("zbank", [128, 512])
        if fwd:
            hout = m.sb("hout", [128, 2, PX])
            hb = m.sb("hb", [128, 2, 8, 128])
            a1 = m.sb("a1", [128, M2, H, 2])
            a2 = m.sb("a2", [128, M2, 128])
            xq = m.sb("xq", [ROWS, 2, M2, 128])
            f1 = m.sb("f1", [128, 48])
            gm = m.sb("gm", [128, ROWS])
            tb = m.ps("tb", [128, 512])
            fbank = m.ps("fbank", [128, 512])
        else:
            hln = m.sb("hln", [128, 2, 512])
            g1 = m.sb("g1", [128, 2, 2, 512])
            g2 = m.sb("g2", [128, 2, 512])
            w1 = m.sb("w1", [128, 128])
            b1 = m.sb("b1", [128, 1])
            w2 = m.sb("w2", [128, 64])
            b2 = m.sb("b2", [128, 1])
            w3 = m.sb("w3", [128, 64])
            b3 = m.sb("b3", [128, 1])
            o1 = m.sb("o1", [128, 2, PX])
            fc1p = m.ps("fc1p", [128, 2, 512])
            fc2p = m.ps("fc2p", [128, 512])
            fc3p = m.ps("fc3p", [128, 512])

        consts_in, zeroed, prepared = m.sem("consts_in"), m.sem("zeroed"), m.sem("prepared")
        conv_made = m.sem("conv_made")
        in_loaded = [m.sem(f"in_loaded{k}") for k in range(2)]
        y_loaded = [m.sem(f"y_loaded{k}") for k in range(2)]
        z_made, z_copied = m.sem("z_made"), m.sem("z_copied")
        acc_made, squared, summed = m.sem("acc_made"), m.sem("squared"), m.sem("summed")
        root_step, norm_made = m.sem("root_step"), m.sem("norm_made")
        ta_made, ln_made = m.sem("ta_made"), m.sem("ln_made")
        if fwd:
            tb_made, hb_copied = m.sem("tb_made"), m.sem("hb_copied")
            f_made, f_copied = m.sem("f_made"), m.sem("f_copied")
            h_stored = [m.sem(f"h_stored{k}") for k in range(2)]
            x_stored = [m.sem(f"x_stored{k}") for k in range(2)]
        else:
            fc1_made, fc1_gelu = m.sem("fc1_made"), m.sem("fc1_gelu")
            fc2_made, fc2_gelu = m.sem("fc2_made"), m.sem("fc2_gelu")
            fc3_made, out_biased = m.sem("fc3_made"), m.sem("out_biased")
            out_stored = [m.sem(f"out_stored{k}") for k in range(2)]

        hsrc, hdst = T["h"][(layer + 1) % 2], T["h"][layer % 2]
        column = lambda v: v.rearrange("(c o) -> c o", o=1)
        loads, late_loads = [(ident[:, :], T["k_ident"])], []
        lng, lnb = (T["ln0_g"], T["ln0_b"]) if first else (T["ln_g"][layer], T["ln_b"][layer])
        for i in range(QI):
            loads += [(gain[C * i:C * i + C, :], column(lng)), (shift[C * i:C * i + C, :], column(lnb))]
        if first:
            loads += [(fc0w[3 * j:3 * j + 3, :], T["fc0_w"]) for j in range(32)]
            loads += [(fc0w[96:97, :], T["fc0_b"].rearrange("(o c) -> o c", o=1)), (mask[:, :], T["k_fc0"])]
        else:
            loads += [(gi[:, :], T["k_gi"]), (emat[:, :, :].rearrange("p a b -> p (a b)"), T["k_e"]),
                      (centre[:, :], T["k_centre"]), (block[:, :, :].rearrange("p a b -> p (a b)"), T["k_block"])]
            loads += [(convrow[C * i:C * i + C, :], T["conv_w"][layer]) for i in range(QI)]
            late_loads += [(biascol[C * i:C * i + C, 96:97], column(T["conv_b"][layer])) for i in range(QI)]
        if fwd:
            loads += [(f1[:, :], T["k_f1"]), (gm[:, :], T["k_g"])]
        else:
            loads += [(w1[C * i:C * i + C, :], T["fc1_w"]) for i in range(QI)]
            loads += [(b1[:, :], column(T["fc1_b"])), (w2[:, :], T["fc2_w"]),
                      (b3[:, :], T["fc3_b"].rearrange("(o c) -> o c", o=1).broadcast_to([128, 1]))]
            loads += [(b2[64 * i:64 * i + 64, :], column(T["fc2_b"])) for i in range(2)]
            late_loads += [(w3[64 * i:64 * i + 64, i:i + 1], T["fc3_w"]) for i in range(2)]
        ALL_IN = 16 * (len(loads) + len(late_loads))
        NPREP = 5
        unit = lambda q, g: q.n * GROUPS + g

        with nc.Block() as blk:
            @blk.sync
            def _(sp):
                for dst, src in loads:
                    sp.dma_start(dst, src).then_inc(consts_in, 16)
                sp.wait_ge(zeroed, 2 if final else 1)
                for dst, src in late_loads:
                    sp.dma_start(dst, src).then_inc(consts_in, 16)

                def load_in(q):
                    if not q.exists:
                        return
                    if first:
                        wait(sp, z_made, (q.n - 2) * ZU + 1)
                        sp.dma_start(xs[:, q.parity, :, :].rearrange("p a b -> p (a b)"), T["x"][q.n]).then_inc(in_loaded[q.parity], 16)
                    else:
                        wait(sp, acc_made, (q.n - 2) * GROUPS + GROUPS)
                        sp.dma_start(hin[:, q.parity, :], hsrc[q.n]).then_inc(in_loaded[q.parity], 16)

                def load_y(q):
                    if not first and q.exists:
                        wait(sp, z_made, (q.n - 2) * ZU + 3)
                        sp.dma_start(yq[:, q.parity, :, :], T["Y"][q.n]).then_inc(y_loaded[q.parity], 16)

                def body(q):
                    if first:
                        load_in(q + 1)
                    else:
                        load_in(q)
                    load_y(q + 1)

                quad_times(sp, body, last=QUADS)

            @blk.gpsimd
            def _(pool):
                fills = [(xt[96:97, :, :, :], 1.0) if first else (biascol[:, :], 0.0)]
                fills += [(w3[:, :], 0.0)] if final else []
                for n, (dst, value) in enumerate(fills):
                    pool.memset(dst, value).then_inc(zeroed, 1)
                    pool.wait_ge(zeroed, n + 1)

            @blk.vector
            def _(dve):
                dve.wait_ge(consts_in, ALL_IN)
                dve.tensor_scalar(gain[:, :], gain[:, :], float(C) ** 0.5, None, ALU.mult).then_inc(prepared, 1)
                if first:
                    dve.tensor_reduce(fc0sum[:, :], fc0w[:, :], AX.X, ALU.add).then_inc(prepared, 1)
                    dve.wait_ge(prepared, 2)
                    dve.tensor_scalar(fc0mean[:, :], fc0sum[:, :], 1.0 / C, None, ALU.mult).then_inc(prepared, 1)
                    dve.wait_ge(prepared, 3)
                    dve.tensor_scalar(fc0c[:, :], fc0w[:, :], fc0mean[:, 0:1], None, ALU.subtract).then_inc(prepared, 1)
                    dve.wait_ge(prepared, 4)
                    dve.tensor_tensor(fc0[:, :, :], mask[:, :].unsqueeze(2).broadcast_to([97, 32, C]),
                                      fc0c[:, :].unsqueeze(1).broadcast_to([97, 32, C]), ALU.mult).then_inc(prepared, 1)
                else:
                    dve.tensor_tensor(convdiag[:, :, :], block[:, :, :],
                                      convrow[:, :].unsqueeze(1).broadcast_to([128, 4, C]), ALU.mult).then_inc(prepared, 1)
                    dve.wait_ge(conv_made, 1)
                    dve.tensor_copy(wconv[:, :], accs[0][:, 0:128]).then_inc(prepared, 1)
                    for p in range(2):
                        dve.tensor_copy(z2[96:97, p, :, :], accs[1][96:97, 0:128].unsqueeze(1).broadcast_to([1, 16, 128])).then_inc(prepared, 1)

                def sums(q, g):
                    if q.exists:
                        at = 16 * (g % BATCH)
                        wait(dve, squared, unit(q, g) + 1)
                        dve.tensor_reduce(ssq[:, (g // BATCH) % 2, at:at + 16], square[:, g % 2, :].rearrange("p (n c) -> p n c", c=C), AX.X,
                                          ALU.add).then_inc(summed, 1)

                def roots(q, b):
                    if not q.exists:
                        return
                    v, y = ssq[:, b % 2, :], rstd[:, b % 2, :]
                    done = (q.n * (GROUPS // BATCH) + b) * ROOT_STEPS
                    wait(dve, summed, unit(q, b * BATCH) + BATCH)
                    dve.tensor_scalar(v, v, C * EPS, None, ALU.add).then_inc(root_step, 1)
                    dve.wait_ge(root_step, done + 1)
                    dve.tensor_scalar(y.bitcast(I32), v.bitcast(I32), -0.5, ROOT_GUESS, ALU.mult, ALU.add).then_inc(root_step, 1)
                    for k in range(2, ROOT_STEPS, 3):
                        dve.wait_ge(root_step, done + k)
                        dve.scalar_tensor_tensor(out=newton[:, :], in0=y, scalar=-0.5, in1=y, op0=ALU.mult, op1=ALU.mult).then_inc(root_step, 1)
                        dve.wait_ge(root_step, done + k + 1)
                        dve.tensor_tensor(newton[:, :], newton[:, :], v, ALU.mult).then_inc(root_step, 1)
                        dve.wait_ge(root_step, done + k + 2)
                        dve.scalar_tensor_tensor(out=y, in0=newton[:, :], scalar=1.5, in1=y, op0=ALU.add, op1=ALU.mult).then_inc(root_step, 1)

                def normalise(q, g):
                    if q.exists:
                        b, at = g // BATCH, 16 * (g % BATCH)
                        if g % BATCH == 0:
                            wait(dve, root_step, (q.n * (GROUPS // BATCH) + b + 1) * ROOT_STEPS)
                        wait(dve, ta_made, unit(q, g) - 1)
                        dve.tensor_tensor(normed[:, g % 2, :].rearrange("p (n c) -> p n c", c=C),
                                          accs[g % NACC][:, :].rearrange("p (n c) -> p n c", c=C),
                                          rstd[:, b % 2, at:at + 16].unsqueeze(2).broadcast_to([128, 16, C]), ALU.mult).then_inc(norm_made, 1)

                def copy_hb(q, g):
                    if q.exists:
                        wait(dve, tb_made, unit(q, g) + 1)
                        wait(dve, f_made, q.n * FU + g // 2 - 1 if g >= 4 else (q.n - 1) * FU + g // 2 + 3)
                        dve.tensor_copy(hb[:, (g // 2) % 2, g % 2::2, :], tb[:, :].rearrange("p (t n) -> p t n", t=4)).then_inc(hb_copied, 1)

                def finish(q, g):
                    if q.exists:
                        wait(dve, fc3_made, unit(q, g) + 1)
                        if g == 0:
                            wait(dve, out_stored[q.parity], q.uses(2) * 32)
                        at = 8 * (g // 2)
                        dst = o1[:, q.parity, at * 128:(at + 8) * 128].rearrange("p (t r n) -> p t r n", r=2, n=128)[:, :, g % 2, :]
                        dve.tensor_scalar(dst, fc3p[:, :].rearrange("p (t n) -> p t n", t=4), b3[:, 0:1], None, ALU.add).then_inc(out_biased, 1)

                def body(q):
                    for s in range(GROUPS):
                        if fwd:
                            copy_hb(*q.back(s, 5))
                            normalise(*q.back(s, 2))
                            sums(q, s)
                            if s % 2 == 1:
                                roots(q, s // 2)
                        else:
                            normalise(*q.back(s, 1))
                            sums(q, s)
                            roots(q, s)
                            finish(*q.back(s, 4))

                quad_times(dve, body, first=0)

            @blk.scalar
            def _(act):
                copy = lambda dst, src: act.activation(dst, src, ACT.Copy)

                def squares(q, g):
                    if q.exists:
                        wait(act, acc_made, unit(q, g) + 1)
                        wait(act, summed, unit(q, g) - 1)
                        act.activation(square[:, g % 2, :], accs[g % NACC][:, :], ACT.Square).then_inc(squared, 1)

                def affine(q, g):
                    if not q.exists:
                        return
                    wait(act, ta_made, unit(q, g) + 1)
                    if fwd:
                        if g == 0:
                            stored(act, h_stored, q, 2)
                            wait(act, tb_made, (q.n - 1) * GROUPS)
                        at = 8 * (g // 2)
                        dst = hout[:, q.parity, at * 128:(at + 8) * 128].rearrange("p (t r n) -> p t r n", r=2, n=128)[:, :, g % 2, :]
                        src = ta[:, :].rearrange("p (t n) -> p t n", t=4)
                    else:
                        wait(act, fc1_made, (unit(q, g) - 1) * 2)
                        dst, src = hln[:, g % 2, :], ta[:, :]
                    fn = ACT.Identity if first or final else ACT.Gelu
                    act.activation(dst, src, fn, bias=shift[:, 0:1], scale=gain[:, 0:1]).then_inc(ln_made, 1)

                def z_copy(q, k):
                    if not q.exists or k >= ZU:
                        return
                    wait(act, z_made, q.n * ZU + k + 1)
                    if first and k == 0:
                        wait(act, z_made, q.n * ZU)
                        copy(xb[:, :, :, :].rearrange("p j i ch -> p ch i j"),
                             zbank[:, 0:384].rearrange("p (ch i j) -> p ch i j", ch=3, i=QI)).then_inc(z_copied, 1)
                    elif first and k == 1:
                        wait(act, acc_made, (q.n - 1) * GROUPS)
                        copy(xt[0:96, q.parity, :, :], zbank[0:96, :].rearrange("p (b n) -> p b n", b=4)).then_inc(z_copied, 1)
                    elif k < 3:
                        copy(z1[:, :, 4 * k:4 * k + 4, :].rearrange("p h k r -> p k h r"),
                             zbank[:, :].rearrange("p (k h r) -> p k h r", k=4, r=2)).then_inc(z_copied, 1)
                    else:
                        wait(act, acc_made, (q.n - 1) * GROUPS)
                        copy(z2[0:96, q.parity, 4 * (k - 3):4 * (k - 3) + 4, :],
                             zbank[0:96, :].rearrange("p (b n) -> p b n", b=4)).then_inc(z_copied, 1)

                def f_copy(q, k):
                    if not q.exists:
                        return
                    wait(act, f_made, q.n * FU + k + 1)
                    if k < 4:
                        copy(a1[:, :, 16 * k:16 * k + 16, :].rearrange("p k h r -> p h k r"),
                             fbank[:, 0:384].rearrange("p (h k r) -> p h k r", k=M2, r=2)).then_inc(f_copied, 1)
                    elif k < 7:
                        copy(a2[:, 4 * (k - 4):4 * (k - 4) + 4, :].rearrange("p k n -> p (k n)"), fbank[:, :]).then_inc(f_copied, 1)
                    else:
                        if k == 7:
                            stored(act, x_stored, q, 2)
                        copy(xq[:, q.parity, 4 * (k - 7):4 * (k - 7) + 4, :].rearrange("p k n -> p (k n)"),
                             fbank[0:ROWS, :]).then_inc(f_copied, 1)
                        if k == FU - 1:
                            wait(act, f_copied, q.n * FU + FU)
                            act.dma_start(T["X"][q.n], xq[:, q.parity, :, :]).then_inc(x_stored[q.parity], 16)

                def store_h(q):
                    if q.exists:
                        wait(act, ln_made, q.n * GROUPS + GROUPS)
                        act.dma_start(hdst[q.n], hout[:, q.parity, :]).then_inc(h_stored[q.parity], 16)

                def gelu1(q, g, pair):
                    if q.exists:
                        n = unit(q, g) * 2 + pair
                        wait(act, fc1_made, n + 1)
                        wait(act, fc2_made, n - 1)
                        act.activation(g1[:, pair, :, :], fc1p[:, :, :], ACT.Gelu, bias=b1[:, 0:1]).then_inc(fc1_gelu, 1)

                def gelu2(q, g, pair):
                    if q.exists:
                        wait(act, fc2_made, unit(q, g) * 2 + pair + 1)
                        wait(act, fc3_made, unit(q, g))
                        act.activation(g2[:, pair, :], fc2p[:, :], ACT.Gelu, bias=b2[:, 0:1]).then_inc(fc2_gelu, 1)

                def store_out(q):
                    if q.exists:
                        wait(act, out_biased, q.n * GROUPS + GROUPS)
                        for pair in range(2):
                            act.dma_start(T["tok"][q.n][2 * pair:2 * pair + 2, :], o1[64 * pair:64 * pair + 2, q.parity, :]).then_inc(out_stored[q.parity], 16)

                def body(q):
                    for s in range(GROUPS):
                        if final:
                            gelu1(*q.back(s, 3), 0)
                            squares(q, s)
                            gelu1(*q.back(s, 3), 1)
                            gelu2(*q.back(s, 3), 0)
                            z_copy(q + 1, s)
                            affine(*q.back(s, 2))
                            gelu2(*q.back(s, 3), 1)
                            if s == 5:
                                store_out(q + -1)
                            continue
                        early, middle, late = forward_units(q, s)
                        squares(q, s)
                        for unit_at in early:
                            f_copy(*unit_at)
                        z_copy(q + 1, s)
                        affine(*q.back(s, 3))
                        if s == 3:
                            store_h(q + -1)
                        for unit_at in middle + late:
                            f_copy(*unit_at)

                act.wait_ge(prepared, NPREP)
                act.wait_ge(consts_in, ALL_IN)
                quad_times(act, body)
                for p in range(2):
                    for sem in ((h_stored[p], x_stored[p]) if fwd else (out_stored[p],)):
                        act.wait_ge(sem, (16 if fwd else 32) * QUADS // 2)

            @blk.tensor
            def _(pe):
                pe.wait_ge(consts_in, ALL_IN)
                pe.wait_ge(zeroed, 2 if final else 1)
                if not first:
                    pe.wait_ge(prepared, 2)
                    pe.matmul(accs[0][:, 0:128], convdiag[:, :, :].rearrange("p a b -> p (a b)"), centre[:, :], start=True, stop=True)
                    pe.matmul(accs[1][0:97, 0:128], biascol[:, :], centre[:, :], start=True, stop=True).then_inc(conv_made, 1)
                pe.wait_ge(prepared, NPREP)

                def prepare(q, k):
                    if not q.exists or k >= ZU:
                        return
                    wait(pe, z_copied, q.n * ZU + k)
                    if first and k == 0:
                        loaded(pe, in_loaded, q)
                        for ch in range(3):
                            mm = pe.transpose(zbank[:, 128 * ch:128 * ch + 128], xs[:, q.parity, :, ch], ident[:, :])
                    elif first and k == 1:
                        for b in range(4):
                            mm = pe.transpose(zbank[0:96, 128 * b:128 * b + 128],
                                              xb[:, 8 * b:8 * b + 8, :, :].rearrange("p j i ch -> p (j i ch)"), ident[:, :])
                    elif k < 3:
                        if k == 0:
                            loaded(pe, y_loaded, q)
                        for d in range(4):
                            mm = pe.matmul(zbank[:, 128 * d:128 * d + 128], yq[:, q.parity, 4 * k + d, :], gi[:, :], start=True, stop=True)
                    else:
                        for d in range(4):
                            b = 4 * (k - 3) + d
                            mm = pe.transpose(zbank[0:96, 128 * d:128 * d + 128],
                                              z1[:, 4 * b:4 * b + 4, :, :].rearrange("p h k r -> p (h k r)"), ident[:, :])
                    mm.then_inc(z_made, 1)

                def accumulate(q, g):
                    if not q.exists:
                        return
                    acc = accs[g % NACC]
                    wait(pe, norm_made, unit(q, g) - NACC + 1)
                    if first:
                        wait(pe, z_copied, q.n * ZU + 2)
                        cols = fc0[:, 16 * (g % 2):16 * (g % 2) + 16, :].rearrange("p n c -> p (n c)")
                        mm = pe.matmul(acc[:, :], xt[:, q.parity, g // 2, :], cols, start=True, stop=True)
                    else:
                        if g == 0:
                            loaded(pe, in_loaded, q)
                            wait(pe, z_copied, q.n * ZU + ZU)
                        gg, par = g // 2, g % 2
                        pe.matmul(acc[:, :], emat[:, par, :], z2[:, q.parity, 4 * gg:4 * gg + 4, :].rearrange("p b n -> p (b n)"),
                                  start=True, stop=False)
                        for t in range(4):
                            j = tile_of(g, t)
                            mm = pe.matmul(acc[:, 128 * t:128 * t + 128], hin[:, q.parity, 128 * j:128 * j + 128], wconv[:, :],
                                           start=False, stop=(t == 3))
                    mm.then_inc(acc_made, 1)

                def to_channels(q, g):
                    if q.exists:
                        wait(pe, norm_made, unit(q, g) + 1)
                        wait(pe, ln_made, unit(q, g))
                        for t in range(4):
                            mm = pe.transpose(ta[:, 128 * t:128 * t + 128], normed[:, g % 2, 128 * t:128 * t + 128], ident[:, :])
                        mm.then_inc(ta_made, 1)

                def to_pixels(q, g):
                    if q.exists:
                        wait(pe, ln_made, unit(q, g) + 1)
                        wait(pe, hb_copied, unit(q, g))
                        for t in range(4):
                            j = tile_of(g, t)
                            mm = pe.transpose(tb[:, 128 * t:128 * t + 128], hout[:, q.parity, 128 * j:128 * j + 128], ident[:, :])
                        mm.then_inc(tb_made, 1)

                def forward(q, k):
                    if not q.exists:
                        return
                    wait(pe, f_copied, q.n * FU + k)
                    if k < 4:
                        wait(pe, hb_copied, q.n * GROUPS + 2 * k + 2)
                        for j in range(8):
                            mm = pe.matmul(fbank[:, 48 * j:48 * j + 48], hb[:, k % 2, j, :], f1[:, :], start=True, stop=True)
                    elif k < 7:
                        for d in range(4):
                            mm = pe.transpose(fbank[:, 128 * d:128 * d + 128], a1[:, 4 * (k - 4) + d, :, :].rearrange("p h r -> p (h r)"), ident[:, :])
                    else:
                        at = 4 * (k - 7)
                        mm = pe.matmul(fbank[0:ROWS, :], gm[:, :], a2[:, at:at + 4, :].rearrange("p k n -> p (k n)"), start=True, stop=True)
                    mm.then_inc(f_made, 1)

                def fc1(q, g, pair):
                    if q.exists:
                        n = unit(q, g) * 2 + pair
                        wait(pe, ln_made, unit(q, g) + 1)
                        wait(pe, fc1_gelu, n)
                        for e in range(2):
                            i = 2 * pair + e
                            mm = pe.matmul(fc1p[:, e, :], w1[C * i:C * i + C, :], hln[C * i:C * i + C, g % 2, :], start=True, stop=True)
                        mm.then_inc(fc1_made, 1)

                def fc2(q, g, pair):
                    if q.exists:
                        n = unit(q, g) * 2 + pair
                        wait(pe, fc1_gelu, n + 1)
                        wait(pe, fc2_gelu, n)
                        for e in range(2):
                            mm = pe.matmul(fc2p[64 * e:64 * e + 64, :], w2[:, :], g1[:, pair, e, :], start=True, stop=True)
                        mm.then_inc(fc2_made, 1)

                def fc3(q, g):
                    if q.exists:
                        wait(pe, fc2_gelu, unit(q, g) * 2 + 2)
                        wait(pe, out_biased, unit(q, g))
                        for pair in range(2):
                            mm = pe.matmul(fc3p[64 * pair:64 * pair + 64, :], w3[:, :], g2[:, pair, :], start=True, stop=True)
                        mm.then_inc(fc3_made, 1)

                def body(q):
                    for s in range(GROUPS):
                        if final:
                            fc1(*q.back(s, 3), 0)
                            accumulate(q, s)
                            fc3(*q.back(s, 4))
                            fc1(*q.back(s, 3), 1)
                            fc2(*q.back(s, 3), 0)
                            prepare(q + 1, s)
                            to_channels(*q.back(s, 2))
                            fc2(*q.back(s, 3), 1)
                            continue
                        early, middle, late = forward_units(q, s)
                        accumulate(q, s)
                        for unit_at in early:
                            forward(*unit_at)
                        prepare(q + 1, s)
                        to_channels(*q.back(s, 3))
                        for unit_at in middle:
                            forward(*unit_at)
                        to_pixels(*q.back(s, 4))
                        for unit_at in late:
                            forward(*unit_at)

                quad_times(pe, body)


def loaded(eng, sems, q):
    eng.wait_ge(sems[q.parity], q.uses(0) * 16)


def stored(eng, sems, q, before):
    wait(eng, sems[q.parity], q.uses(before) * 16)


def mix_pass(nc, layer, T):
    with ExitStack() as ctx:
        m = Store(nc, ctx, f"m{layer}")
        ident = m.sb("ident", [128, 128])
        raw = m.sb("raw", [128, 2, C, M1 * M2])
        mean = m.sb("mean", [128, 2, M1 * M2])
        wk = m.sb("wk", [128, 2, M1, 2, C])
        xi = m.sb("xi", [128, 2, M1, 128])
        xt = m.sb("xt", [128, 2, M1, 128])
        yo = m.sb("yo", [128, 2, M1, 2, 64])
        turned = m.ps("turned", [128, 3, 512])
        prod = [m.ps(f"prod{s}", [128, 2, 512]) for s in range(2)]
        consts_in, negated, summed, centred = m.sem("consts_in"), m.sem("negated"), m.sem("summed"), m.sem("centred")
        x_in = [m.sem(f"x_in{k}") for k in range(2)]
        y_out = [m.sem(f"y_out{k}") for k in range(2)]
        w_cut, x_turned, x_copied = m.sem("w_cut"), m.sem("x_turned"), m.sem("x_copied")
        mixed, y_copied = m.sem("mixed"), m.sem("y_copied")
        flat = raw[:, :, :, :].rearrange("p r c m -> p r (c m)")
        with nc.Block() as blk:
            @blk.sync
            def _(sp):
                sp.dma_start(ident[:, :], T["k_ident"]).then_inc(consts_in, 16)
                for side, (wr, wi) in enumerate((("w1r", "w1i"), ("w2r", "w2i"))):
                    for rin in range(2):
                        p = 64 * side + 32 * rin
                        for rout in range(2):
                            src = T[wi if rin != rout else wr][layer].rearrange("i o x y -> i (o x y)")
                            sp.dma_start(flat[p:p + 32, rout, :], src).then_inc(consts_in, 16)
                with sp.Fori(0, M2 // 2) as i:
                    for u in range(2):
                        sp.wait_ge(x_turned, i * 2 + u + 1)
                        sp.dma_start(xi[:, u, :, :].rearrange("p k n -> p (k n)").rearrange("p (r c) -> p r c", c=C),
                                     T["Xk"][i * 2 + u]).then_inc(x_in[u], 16)

            @blk.gpsimd
            def _(pool):
                pool.wait_ge(centred, 2)
                with pool.Fori(0, M2 // 2) as i:
                    for u in range(2):
                        ky = i * 2 + u
                        pool.wait_ge(mixed, ky + 1)
                        pool.tensor_copy(wk[:, u, :, :, :],
                                         raw[:, :, :, :].rearrange("p r c (x y) -> p x r c y", y=M2)[:, :, :, :, bass.ds(ky, 1)].rearrange("p x r c y -> p x r (c y)")).then_inc(w_cut, 1)

            @blk.vector
            def _(dve):
                dve.wait_ge(consts_in, 16 * 9)
                for side in range(2):
                    p = 64 * side + 32
                    mm = dve.tensor_scalar(flat[p:p + 32, 0, :], flat[p:p + 32, 0, :], -1.0, None, ALU.mult)
                    mm.then_inc(negated, 1)
                dve.wait_ge(negated, 2)
                dve.tensor_reduce(mean[:, :, :], raw[:, :, :, :].rearrange("p r c m -> p r m c"), AX.X, ALU.add).then_inc(summed, 1)
                dve.wait_ge(summed, 1)
                for rout in range(2):
                    dve.scalar_tensor_tensor(out=raw[:, rout, :, :], in0=mean[:, rout, :].unsqueeze(1).broadcast_to([128, C, M1 * M2]),
                                             scalar=-1.0 / C, in1=raw[:, rout, :, :], op0=ALU.mult, op1=ALU.add).then_inc(centred, 1)
                with dve.Fori(0, M2 // 2) as i:
                    for u in range(2):
                        ky = i * 2 + u
                        dve.wait_ge(mixed, ky + 1)
                        dve.wait_ge(x_turned, ky + 3)
                        for b in range(3):
                            mm = dve.tensor_copy(xt[:, u, 4 * b:4 * b + 4, :].rearrange("p k n -> p (k n)"), turned[:, b, :])
                        mm.then_inc(x_copied, 1)

            @blk.scalar
            def _(act):
                act.sem_inc(y_copied, 1)
                with act.Fori(0, M2 // 2) as i:
                    for u in range(2):
                        ky = i * 2 + u
                        act.wait_ge(mixed, ky + 3)
                        act.wait_ge(y_out[u], i * 16 + 16)
                        for side in range(2):
                            for b, k in ((0, 8), (1, 4)):
                                mm = act.activation(yo[:, u, 8 * b:8 * b + k, side, :],
                                                    prod[side][:, b, 0:64 * k].rearrange("p (k n) -> p k n", n=64), ACT.Copy)
                        mm.then_inc(y_copied, 1)
                        act.wait_ge(y_copied, ky + 2)
                        act.dma_start(T["Yk"][ky], yo[:, u, :, :, :].rearrange("p k s n -> p (k s n)").rearrange("p (r c) -> p r c", c=C)).then_inc(y_out[u], 16)
                for u in range(2):
                    act.wait_ge(y_out[u], 16 * (M2 // 2 + 1))

            @blk.tensor
            def _(pe):
                pe.sem_inc(x_turned, 2)
                pe.sem_inc(mixed, 2)
                pe.sem_inc(y_out[0], 16)
                pe.sem_inc(y_out[1], 16)
                pe.sem_inc(x_copied, 1)
                pe.wait_ge(consts_in, 16 * 9)

                def turn(i, u):
                    pe.wait_ge(x_in[u], i * 16 + 16)
                    pe.wait_ge(x_copied, i * 2 + u + 1)
                    for k in range(M1):
                        mm = pe.transpose(turned[:, k // 4, 128 * (k % 4):128 * (k % 4) + 128], xi[:, u, k, :], ident[:, :])
                    mm.then_inc(x_turned, 1)

                def mix(i, u):
                    ky = i * 2 + u
                    pe.wait_ge(x_copied, ky + 2)
                    pe.wait_ge(w_cut, ky + 1)
                    pe.wait_ge(y_copied, ky + 1)
                    for k in range(M1):
                        for side in range(2):
                            p = 64 * side
                            mm = pe.matmul(prod[side][:, k // 8, 64 * (k % 8):64 * (k % 8) + 64], xt[p:p + 64, u, k, :],
                                           wk[p:p + 64, u, k, :, :].rearrange("p r c -> p (r c)"), start=True, stop=True)
                    mm.then_inc(mixed, 1)

                turn(0, 0)
                with pe.Fori(0, M2 // 2 - 1) as i:
                    turn(i, 1)
                    mix(i, 0)
                    turn(i + 1, 0)
                    mix(i, 1)
                turn(M2 // 2 - 1, 1)
                mix(M2 // 2 - 1, 0)
                mix(M2 // 2 - 1, 1)


def layer_norm_rows(dve, pool, m, src, dst, sums, tmp, step, rooted, consts, base=0):
    n, w = src.shape[1], src.shape[2]
    wide = lambda v: v.unsqueeze(2).broadcast_to([128, n, w])
    if pool is not None:
        pool.wait_ge(step, base + 6)
        pool.tensor_tensor(sums[:, 2, :], sums[:, 1, :], consts[:, 0, :], ALU.pow).then_inc(rooted, 1)
        return
    ops = [lambda: dve.tensor_reduce(sums[:, 0, :], src, AX.X, ALU.add),
           lambda: dve.tensor_scalar(sums[:, 0, :], sums[:, 0, :], 1.0 / w, None, ALU.mult),
           lambda: dve.tensor_tensor(dst, src, wide(sums[:, 0, :]), ALU.subtract),
           lambda: dve.tensor_tensor(tmp, dst, dst, ALU.mult),
           lambda: dve.tensor_reduce(sums[:, 1, :], tmp, AX.X, ALU.add),
           lambda: dve.tensor_scalar(sums[:, 1, :], sums[:, 1, :], 1.0 / w, EPS, ALU.mult, ALU.add)]
    for k, op in enumerate(ops):
        if base + k:
            dve.wait_ge(step, base + k)
        op().then_inc(step, 1)
    dve.wait_ge(rooted, 1)
    dve.tensor_tensor(dst, dst, wide(sums[:, 2, :]), ALU.mult).then_inc(step, 1)
    return base + 7


def attention_pass(nc, T):
    KT, QB = H, IMAGES * H // 512
    with ExitStack() as ctx:
        m = Store(nc, ctx, "at")
        ident = m.sb("ident", [128, 128])
        y = m.sb("y", [128, H, W])
        f2 = m.sb("f2", [128, H, 2, W], F32R)
        ft = m.sb("ft", [128, H, 128], F32R)
        fts = m.sb("fts", [128, H, 128], F32R)
        sums = m.sb("sums", [128, 6, H])
        consts = m.sb("consts", [128, 2, H])
        qs = m.sb("qs", [128, 2, 512], F32R)
        p = m.sb("p", [128, 4, 1024])
        tmp = p[:, :, :].rearrange("p a (b w) -> p (a b) w", w=W)
        p_hi = m.sb("p_hi", [128, 4, 1024], F32R)
        p_lo = m.sb("p_lo", [128, 4, 1024], F32R)
        dens = m.sb("dens", [128, H, QB])
        ot = m.sb("ot", [128, 2, 512])
        score = [m.ps(f"score{k}", [128, 2, 512]) for k in range(2)]
        acc = [m.ps(f"acc{k}", [128, 512]) for k in range(2)]
        back = m.ps("back", [128, 512])
        o = y
        den = m.sb("den", [128, H])

        loaded_in, zeroed, step, rooted = m.sem("loaded_in"), m.sem("zeroed"), m.sem("step"), m.sem("rooted")
        turned, turn_copied = m.sem("turned"), m.sem("turn_copied")
        q_copied, scored, exped, summed = m.sem("q_copied"), m.sem("scored"), m.sem("exped"), m.sem("summed")
        hi_even, hi_odd, lo_made = m.sem("hi_even"), m.sem("hi_odd"), m.sem("lo_made")
        acc_copied, o_turned, o_copied, stored_out = m.sem("acc_copied"), m.sem("o_turned"), m.sem("o_copied"), m.sem("stored_out")
        NP = KT // 2
        PRE = 14
        FINAL = PRE + 12

        def blocks(eng, body):
            for b in range(2):
                body(b, b)
            with eng.Fori(1, QB // 2 - 1) as i:
                for u in range(2):
                    body(i * 2 + u, u)
            for b in range(QB - 2, QB):
                body(b, b % 2)

        is_last = lambda b: isinstance(b, int) and b == QB - 1
        is_first = lambda b: isinstance(b, int) and b == 0

        def split_hi(eng, copy, b, k, made):
            n = b * NP + k
            wait(eng, exped, n * 2 + 2)
            wait(eng, summed, n - 3)
            copy(p_hi[:, k % 4, :], p[:, k % 4, :]).then_inc(made, 1)

        with nc.Block() as blk:
            @blk.sync
            def _(sp):
                sp.dma_start(y[:, :, :], T["tok_rows"]).then_inc(loaded_in, 16)
                sp.dma_start(ident[:, :], T["k_ident"]).then_inc(loaded_in, 16)
                sp.wait_ge(step, PRE + 8)
                sp.dma_start(tmp, T["tok_rows"]).then_inc(loaded_in, 16)
                sp.wait_ge(step, FINAL)
                sp.dma_start(T["att_rows"], tmp).then_inc(stored_out, 16)
                sp.wait_ge(stored_out, 16)

            @blk.gpsimd
            def _(pool):
                pool.memset(consts[:, 0, :], -0.5).then_inc(zeroed, 1)
                pool.wait_ge(zeroed, 1)
                pool.memset(consts[:, 1, :], 0.5).then_inc(zeroed, 1)
                pool.wait_ge(zeroed, 2)
                layer_norm_rows(None, pool, m, y[:, :, :], y, sums, tmp, step, rooted, consts)
                pool.wait_ge(step, 9)
                pool.tensor_tensor(sums[:, 4, :], sums[:, 3, :], consts[:, 1, :], ALU.pow).then_inc(rooted, 1)
                pool.wait_ge(step, PRE + 8)
                pool.tensor_tensor(sums[:, 4, :], sums[:, 3, :], consts[:, 1, :], ALU.pow).then_inc(rooted, 1)

            @blk.vector
            def _(dve):
                wide = lambda v: v.unsqueeze(2).broadcast_to([128, H, W])
                taken = [0]

                def then(ins, wait_next=True):
                    taken[0] += 1
                    ins.then_inc(step, 1)
                    if wait_next:
                        dve.wait_ge(step, taken[0])

                dve.wait_ge(loaded_in, 32)
                dve.wait_ge(zeroed, 2)
                taken[0] = layer_norm_rows(dve, None, m, y[:, :, :], y[:, :, :], sums, tmp, step, rooted, consts)
                dve.wait_ge(step, taken[0])

                def lengths(src):
                    then(dve.tensor_tensor(tmp, src, src, ALU.mult))
                    then(dve.tensor_reduce(sums[:, 3, :], tmp, AX.X, ALU.add))

                def inverse(n):
                    dve.wait_ge(rooted, n)
                    then(dve.tensor_scalar(sums[:, 4, :], sums[:, 4, :], 1e-12, None, ALU.max))
                    then(dve.reciprocal(sums[:, 5, :], sums[:, 4, :]))

                lengths(y[:, :, :])
                inverse(2)
                then(dve.tensor_tensor(y[:, :, :], y[:, :, :], wide(sums[:, 5, :]), ALU.mult))
                then(dve.tensor_copy(f2[:, :, 0, :], y[:, :, :]))
                then(dve.tensor_tensor(f2[:, :, 1, :], y[:, :, :], f2[:, :, 0, :].bitcast(F32), ALU.subtract))
                for b in range(H // 4):
                    dve.wait_ge(turned, b + 1)
                    turn = score[b % 2][:, 0, :]
                    out = [v[:, 4 * b:4 * b + 4, :].rearrange("p t n -> p (t n)") for v in (ft, fts)]
                    dve.tensor_copy(out[0], turn).then_inc(turn_copied, 1)
                    dve.tensor_copy(out[1][0:W, :], turn[W:2 * W, :]).then_inc(turn_copied, 1)
                    dve.tensor_copy(out[1][W:2 * W, :], turn[0:W, :]).then_inc(turn_copied, 1)
                dve.wait_ge(turn_copied, 3 * H // 4)

                def cut(b, u):
                    dve.tensor_copy(qs[:, u, :], ft[:, :, :].rearrange("p t n -> p (t n)")[:, bass.ds(b * 512, 512)]).then_inc(q_copied, 1)

                def put_back(b):
                    wait(dve, o_turned, b + 1)
                    src = back[:, :].rearrange("p (t a w) -> p t a w", a=2, w=W)
                    dve.tensor_copy(o[:, bass.ds(b * 4, 4), :], src[:, :, 0, :]).then_inc(o_copied, 1)
                    dve.wait_ge(o_copied, b * 2 + 1)
                    dve.tensor_tensor(o[:, bass.ds(b * 4, 4), :], o[:, bass.ds(b * 4, 4), :], src[:, :, 1, :], ALU.add).then_inc(o_copied, 1)

                def acc_out(b, u):
                    wait(dve, summed, b * NP + NP)
                    wait(dve, o_turned, b - 1)
                    dve.tensor_copy(ot[:, u, :], acc[u][:, :]).then_inc(acc_copied, 1)

                def split_lo(b, k):
                    n = b * NP + k
                    wait(dve, hi_odd if k % 2 else hi_even, b * (NP // 2) + k // 2 + 1)
                    dve.tensor_tensor(p_lo[:, k % 4, :], p[:, k % 4, :], p_hi[:, k % 4, :].bitcast(F32), ALU.subtract).then_inc(lo_made, 1)

                def body(b, u):
                    for k in range(NP):
                        if k % 2:
                            split_hi(dve, dve.tensor_copy, b, k, hi_odd)
                        split_lo(b, k)
                        if k == 4 and not is_first(b):
                            acc_out(b - 1, 1 - u)
                        if k == 10 and not is_first(b):
                            put_back(b - 1)
                        if k == 14 and not is_last(b):
                            cut(b + 1, 1 - u)

                cut(0, 0)
                blocks(dve, body)
                acc_out(QB - 1, 1)
                put_back(QB - 1)
                dve.wait_ge(o_copied, 2 * QB)
                dve.wait_ge(exped, 2 * QB * NP)
                then(dve.tensor_reduce(sums[:, 1, :], dens[:, :, :], AX.X, ALU.add))
                then(dve.reciprocal(sums[:, 0, :], sums[:, 1, :]))
                then(dve.tensor_scalar(sums[:, 1, :], sums[:, 0, :], 0.2, None, ALU.mult))
                then(dve.tensor_tensor(o[:, :, :], o[:, :, :], wide(sums[:, 1, :]), ALU.mult))
                for part in range(2):
                    then(dve.scalar_tensor_tensor(out=o[:, :, :], in0=f2[:, :, part, :].bitcast(F32), scalar=0.8, in1=o[:, :, :],
                                                  op0=ALU.mult, op1=ALU.add))
                lengths(o[:, :, :])
                inverse(3)
                then(dve.tensor_tensor(o[:, :, :], o[:, :, :], wide(sums[:, 5, :]), ALU.mult))
                dve.wait_ge(loaded_in, 48)
                then(dve.tensor_tensor(tmp, tmp, o[:, :, :], ALU.add))

            @blk.scalar
            def _(act):
                def body(b, u):
                    for k in range(NP):
                        n = b * NP + k
                        wait(act, scored, n + 1)
                        wait(act, lo_made, n - 3)
                        for e in range(2):
                            t = 2 * k + e
                            act.activation(p[:, k % 4, 512 * e:512 * e + 512], score[k % 2][:, e, :], ACT.Exp,
                                           accum_out=dens[:, t, bass.ds(b, 1)]).then_inc(exped, 1)
                        if k % 2 == 0:
                            split_hi(act, lambda dst, src: act.activation(dst, src, ACT.Copy), b, k, hi_even)

                blocks(act, body)

            @blk.tensor
            def _(pe):
                pe.wait_ge(loaded_in, 32)
                pe.wait_ge(step, PRE)
                for b in range(H // 4):
                    if b >= 2:
                        pe.wait_ge(turn_copied, 3 * b - 3)
                    for d in range(4):
                        mm = pe.transpose(score[b % 2][:, 0, 128 * d:128 * d + 128],
                                          f2[:, 4 * b + d, :, :].rearrange("p c w -> p (c w)").bitcast(F32), ident[:, :])
                    mm.then_inc(turned, 1)
                pe.wait_ge(turn_copied, 3 * H // 4)

                def scores(b, u, k):
                    n = b * NP + k
                    if k == 0:
                        wait(pe, q_copied, b + 1)
                    wait(pe, exped, n * 2 - 2)
                    for e in range(2):
                        for keys in (ft, fts):
                            mm = pe.matmul(score[k % 2][:, e, :], keys[:, 2 * k + e, :], qs[:, u, :], start=(keys is ft), stop=(keys is fts))
                    mm.then_inc(scored, 1)

                def weighted(b, u, k):
                    n = b * NP + k
                    wait(pe, lo_made, n + 1)
                    if k == 0:
                        wait(pe, acc_copied, b - 1)
                    for e in range(2):
                        t = 2 * k + e
                        for part in (p_hi, p_lo):
                            mm = pe.matmul(acc[u][:, :], f2[:, t, :, :].rearrange("p c w -> p (c w)"), part[:, k % 4, 512 * e:512 * e + 512],
                                           start=(t == 0 and part is p_hi), stop=(t == KT - 1 and part is p_lo))
                    mm.then_inc(summed, 1)

                def turn_back(b, u):
                    wait(pe, acc_copied, b + 1)
                    wait(pe, o_copied, b * 2)
                    for d in range(4):
                        mm = pe.transpose(back[:, 128 * d:128 * d + 128], ot[:, u, 128 * d:128 * d + 128], ident[:, :])
                    mm.then_inc(o_turned, 1)

                LAG = 3

                def body(b, u):
                    for k in range(NP):
                        scores(b, u, k)
                        if k >= LAG:
                            weighted(b, u, k - LAG)
                        elif not is_first(b):
                            weighted(b - 1, 1 - u, NP + k - LAG)
                        if k == 10 and not is_first(b):
                            turn_back(b - 1, 1 - u)

                blocks(pe, body)
                for k in range(NP - LAG, NP):
                    weighted(QB - 1, 1, k)
                turn_back(QB - 1, 1)


HEADS, DIM, NKEYS, TOPK = 8, 64, 64, 16
NKV = NKEYS * NKEYS
KCH = NKV // 128
TT = IMAGES * H // 128
LOWEST = -3.0e38
BLOCKS = TT // 4
LAG = 3


def ffn_prepare(nc, T):
    with ExitStack() as ctx:
        m = Store(nc, ctx, "fp")
        ident = m.sb("ident", [128, 128])
        h = m.sb("h", [128, TT, W])
        y = m.sb("y", [128, TT, W])
        tmp = m.sb("tmp", [128, TT, W])
        xt = m.sb("xt", [W, TT, 128])
        sums = m.sb("sums", [128, 3, TT])
        consts = m.sb("consts", [128, 1, TT])
        wq = m.sb("wq", [DIM, 4, 128])
        keys = m.sb("keys", [NKEYS, 4, 128])
        wqt = m.sb("wqt", [128, 4, DIM])
        keyst = m.sb("keyst", [128, 4, NKEYS])
        both = m.sb("both", [DIM, HEADS, 2, NKEYS])
        bank = [m.ps(f"bank{k}", [128, 512]) for k in range(2)]
        wbank = [m.ps(f"wbank{k}", [128, 512]) for k in range(4)]
        loaded_in, zeroed, step, rooted = m.sem("loaded_in"), m.sem("zeroed"), m.sem("step"), m.sem("rooted")
        turned, copied = m.sem("turned"), m.sem("copied")
        w_turned, w_copied, w_made, both_copied, stored_out = (m.sem("w_turned"), m.sem("w_copied"), m.sem("w_made"),
                                                               m.sem("both_copied"), m.sem("stored_out"))
        with nc.Block() as blk:
            @blk.sync
            def _(sp):
                sp.dma_start(h[:, :, :], T["att_tiles"]).then_inc(loaded_in, 16)
                sp.dma_start(ident[:, :], T["k_ident"]).then_inc(loaded_in, 16)
                sp.dma_start(wq[:, :, :].rearrange("p a b -> p (a b)"), T["Wq_pk"]).then_inc(loaded_in, 16)
                for p in range(2):
                    sp.dma_start(keys[:, 2 * p:2 * p + 2, :].rearrange("k a b -> k (a b)"),
                                 T["pk_keys"][p].rearrange("k h d -> k (h d)")).then_inc(loaded_in, 16)
                sp.wait_ge(both_copied, 4)
                sp.dma_start(T["both"], both[:, :, :, :].rearrange("d h p k -> d h (p k)")).then_inc(stored_out, 16)
                sp.wait_ge(copied, TT // 4)
                sp.dma_start(T["xt"], xt[:, :, :]).then_inc(stored_out, 16)
                sp.wait_ge(stored_out, 32)

            @blk.gpsimd
            def _(pool):
                pool.memset(consts[:, 0, :], -0.5).then_inc(zeroed, 1)
                pool.wait_ge(zeroed, 1)
                layer_norm_rows(None, pool, m, y[:, :, :], y, sums, tmp, step, rooted, consts)

            @blk.vector
            def _(dve):
                dve.wait_ge(loaded_in, 16 * 5)
                dve.wait_ge(w_turned, 1)
                dve.tensor_copy(wqt[:, :, :].rearrange("p c d -> p (c d)"), wbank[0][:, 0:256]).then_inc(w_copied, 1)
                dve.wait_ge(w_turned, 2)
                dve.tensor_copy(keyst[:, :, :].rearrange("p c k -> p (c k)"), wbank[1][:, 0:256]).then_inc(w_copied, 1)
                dve.wait_ge(w_made, 1)
                for hh in range(4):
                    dve.tensor_copy(both[:, hh::4, :, :].rearrange("d a p k -> d p a k"),
                                    wbank[hh][0:DIM, 0:256].rearrange("d (p a k) -> d p a k", p=2, a=2)).then_inc(both_copied, 1)
                layer_norm_rows(dve, None, m, h[:, :, :], y[:, :, :], sums, tmp[:, :, :], step, rooted, consts)
                for b in range(TT // 4):
                    dve.wait_ge(turned, b + 1)
                    dve.tensor_copy(xt[:, 4 * b:4 * b + 4, :].rearrange("p t n -> p (t n)"), bank[b % 2][0:W, :]).then_inc(copied, 1)

            @blk.tensor
            def _(pe):
                pe.wait_ge(loaded_in, 16 * 5)
                for src, dst in ((wq, wbank[0]), (keys, wbank[1])):
                    for c in range(4):
                        mm = pe.transpose(dst[:, 64 * c:64 * c + 64], src[:, c, :], ident[0:64, 0:64])
                    mm.then_inc(w_turned, 1)
                pe.wait_ge(w_copied, 2)
                for c in range(4):
                    for hh in range(4):
                        rows = slice(32 * hh, 32 * hh + 32)
                        mm = pe.matmul(wbank[hh][0:DIM, 64 * c:64 * c + 64], wqt[rows, c, :], keyst[rows, c, :], start=True, stop=True)
                mm.then_inc(w_made, 1)
                pe.wait_ge(step, 7)
                for b in range(TT // 4):
                    if b >= 2:
                        pe.wait_ge(copied, b - 1)
                    for d in range(4):
                        mm = pe.transpose(bank[b % 2][0:W, 128 * d:128 * d + 128], y[:, 4 * b + d, :], ident[:, :])
                    mm.then_inc(turned, 1)


class Block:

    def __init__(self, pair, u, half, parity, place=None, exists=True):
        self.pair, self.u, self.half, self.parity, self.place, self.exists = pair, u, half, parity, place, exists

    @staticmethod
    def at(pair, place):
        carry, inside = divmod(place, 2 * BLOCKS)
        fixed = isinstance(pair, int)
        exists = place >= 0 and not (fixed and pair + carry >= HEADS // 2)
        block = Block(pair + carry if carry else pair, inside // BLOCKS, inside % BLOCKS // 2, inside % 2, inside, exists)
        block.origin = (pair, place)
        return block

    @property
    def number(self):
        return self.half * 2 + self.parity

    @property
    def n(self):
        return (self.pair * 2 + self.u) * BLOCKS + self.number

    @property
    def uses(self):
        return (self.pair * 2 + self.u) * (BLOCKS // 2) + self.half + 1

    @property
    def opens_head(self):
        return self.place is not None and self.place % BLOCKS == 0

    def __add__(self, d):
        if self.place is not None:
            pair, place = self.origin
            return Block.at(pair, place + d)
        carry, parity = divmod(self.parity + d, 2)
        return Block(self.pair, self.u, self.half + carry, parity)


def block_times(eng, body):
    def pair_times(pair):
        for u in range(2):
            with eng.Fori(1, BLOCKS // 2 - 1) as half:
                for parity in range(2):
                    body(Block(pair, u, half, parity))
            for d in (-2, -1, 0, 1):
                body(Block.at(pair, (u + 1) * BLOCKS + d))

    for place in (-1, 0, 1):
        body(Block.at(0, place))
    with eng.Fori(0, HEADS // 2 - 1) as pair:
        pair_times(pair)
    pair_times(HEADS // 2 - 1)


START = 128


def wait_n(eng, sem, value):
    eng.wait_ge(sem, value + START)


def own_step(eng, sem, value):
    eng.wait_ge(sem, value + START)
    eng.nop(nofuse=True)


def front_events(block, k, step):
    return [(block + 1, j) for j in range(4) if 6 * j + step == k and (block + 1).exists]


def tail_events(block, k, step):
    found = []
    for j in range(4):
        late, at = divmod(4 + 8 * j + step, KCH)
        b = block + (-1 - late)
        if at == k and b.exists:
            found.append((b, j))
    return found


def ffn_pass(nc, T):
    with ExitStack() as ctx:
        m = Store(nc, ctx, "ff")
        ident = m.sb("ident", [128, 128])
        causal = m.sb("causal", [128, 128])
        out = m.sb("out", [128, TT, W])
        table = m.sb("table", [128, 2, KCH, 2 * DIM])
        both = m.sb("both", [DIM, 2, 128])
        wq = m.sb("wq", [DIM, 2, DIM])
        wo = m.sb("wo", [DIM, 2, DIM])
        pick_in = m.sb("pick_in", [128, 8 * 128])
        pick = m.sb("pick", [128, 8, 128], F32R)
        minus8 = m.sb("minus8", [128, 1])
        x = m.sb("x", [DIM, 2, 512])
        sim = m.sb("sim", [128, 2, 2, NKEYS])
        q = m.sb("q", [DIM, 2, 512])
        q2 = m.sb("q2", [DIM, 512])
        cut = m.sb("cut", [128, 2, NKEYS])
        cand_cut = m.sb("cand_cut", [128, TOPK * TOPK])
        best = m.sb("best", [128, 2, TOPK])
        cand = m.sb("cand", [128, TOPK, TOPK])
        top = m.sb("top", [128, TOPK])
        size = m.sb("size", [128, 2])
        thr = m.sb("thr", [128, 4])
        nthr = m.sb("nthr", [128, 1])
        topexp = m.sb("topexp", [128, TOPK])
        total = m.sb("total", [128, 2, 4])
        inv = m.sb("inv", [128, 4])
        z = m.sb("z", [128, 2, 2, 2, 2, 32], F32R)
        zt = m.sb("zt", [128, 2, 4, 512], F32R)
        e = m.sb("e", [128, 4, 512])
        w = m.sb("w", [128, 4, 512])
        kvt = m.sb("kvt", [128, 512])
        kv = m.sb("kv", [128, 2, 2 * DIM])
        kt = m.sb("kt", [DIM, 2, 128])
        att = m.sb("att", [128, 2, 128])
        amax = m.sb("amax", [128, 2, 2])
        prob = m.sb("prob", [128, 2, 128])
        rowsum = m.sb("rowsum", [128, 2, 2])
        probn = m.sb("probn", [128, 2, 128])
        probt = m.sb("probt", [128, 2, 128])
        ot = m.sb("ot", [DIM, 2, 128])
        sump = [m.ps(f"sump{k}", [128, 512]) for k in range(3)]
        kvp = m.ps("kvp", [128, 512])
        simp = m.ps("simp", [128, 512])
        zbank = m.ps("zbank", [128, 512])
        tailp = [m.ps(f"tailp{k}", [128, 512]) for k in range(2)]

        consts_in, picked, filled = m.sem("consts_in"), m.sem("picked"), m.sem("filled")
        head_in = [m.sem(f"head_in{k}") for k in range(2)]
        x_in = [m.sem(f"x_in{k}") for k in range(2)]
        sim_made, sim_copied, q_copied, q2_copied = m.sem("sim_made"), m.sem("sim_copied"), m.sem("q_copied"), m.sem("q2_copied")
        cand_made, thr_step = m.sem("cand_made"), m.sem("thr_step")
        top_step, topped, exped_top, shifted = m.sem("top_step"), m.sem("topped"), m.sem("exped_top"), m.sem("shifted")
        hi_cut, lo_cut, z_turned, zt_copied = m.sem("hi_cut"), m.sem("lo_cut"), m.sem("z_turned"), m.sem("zt_copied")
        summed, exped, masked, kv_made = m.sem("summed"), m.sem("exped"), m.sem("masked"), m.sem("kv_made")
        kvt_copied, kv_turned, inverted = m.sem("kvt_copied"), m.sem("kv_turned"), m.sem("inverted")
        kv_scaled, kt_made, kt_copied = m.sem("kv_scaled"), m.sem("kt_made"), m.sem("kt_copied")
        att_made, att_masked, att_max, att_neg = m.sem("att_made"), m.sem("att_masked"), m.sem("att_max"), m.sem("att_neg")
        att_exp, att_inv, att_scaled = m.sem("att_exp"), m.sem("att_inv"), m.sem("att_scaled")
        probt_made, probt_copied, ot_made, ot_copied = m.sem("probt_made"), m.sem("probt_copied"), m.sem("ot_made"), m.sem("ot_copied")
        o_made, o_added, stored_out = m.sem("o_made"), m.sem("o_added"), m.sem("stored_out")
        HEAD_LOADS = 4 * 2 * 2 + 3
        TOP_STEPS = 10
        cols = lambda j: slice(128 * j, 128 * j + 128)
        tile = lambda b, j: b.n * 4 + j
        halves = [lambda v: v[:, 0, :].rearrange("p (h k) -> p h k", h=2).unsqueeze(2).broadcast_to([128, 2, 2, 32]),
                  lambda v: v[:, 1, :].rearrange("p (h k) -> p h k", h=2).unsqueeze(1).broadcast_to([128, 2, 2, 32])]

        with nc.Block() as blk:
            @blk.sync
            def _(sp):
                for sem in m.sems:
                    sp.sem_inc(sem, START)

        with nc.Block() as blk:
            @blk.sync
            def _(sp):
                sp.dma_start(ident[:, :], T["k_ident"]).then_inc(consts_in, 16)
                sp.dma_start(causal[:, :], T["k_causal"]).then_inc(consts_in, 16)
                sp.dma_start(pick_in[:, :], T["k_pick"]).then_inc(consts_in, 16)
                sp.dma_start(out[:, :, :], T["att_tiles"]).then_inc(consts_in, 16)

                def load_head(pair, u):
                    head = pair * 2 + u
                    wait_n(sp, o_added, (head - 1) * TT)
                    for b in range(4):
                        for half in range(2):
                            at = 16 * half
                            rows = slice(32 * b, 32 * b + 32)
                            sp.dma_start(table[rows, u, at:at + 16, 0:DIM], T["keys_chunks"][head][b][half]).then_inc(head_in[u], 16)
                            sp.dma_start(table[rows, u, at:at + 16, DIM:2 * DIM], T["values_chunks"][head][b][half]).then_inc(head_in[u], 16)
                    sp.dma_start(both[:, u, :], T["both_heads"][head]).then_inc(head_in[u], 16)
                    sp.dma_start(wq[:, u, :], T["Wq_heads"][head]).then_inc(head_in[u], 16)
                    sp.dma_start(wo[:, u, :], T["Wo_heads"][head]).then_inc(head_in[u], 16)

                def body(b):
                    nb = b + 1
                    if nb.exists:
                        wait_n(sp, sim_made, (nb.n - 1) * 4)
                        sp.dma_start(x[:, nb.parity, :], T["xt_blocks"][nb.number]).then_inc(x_in[nb.parity], 16)
                    if b.place == 1 and b.exists:
                        load_head(b.pair, 1)
                    if b.place == BLOCKS + 1 and not isinstance(b.pair, int):
                        load_head(b.pair + 1, 0)

                load_head(0, 0)
                block_times(sp, body)
                wait_n(sp, o_added, HEADS * TT)
                sp.dma_start(T["out_tiles"], out[:, :, :]).then_inc(stored_out, 16)
                wait_n(sp, stored_out, 16)

            @blk.gpsimd
            def _(pool):
                pool.memset(minus8[:, :], -8.0).then_inc(filled, 1)

                def lower_parts(b, j):
                    n = tile(b, j)
                    v = z[:, :, :, :, :, :]
                    for side in range(2):
                        wait_n(pool, hi_cut, n * 2 + 1 + side)
                        pool.tensor_tensor(v[:, :, :, 1, side, :], halves[side](sim[:, j % 2, :, :]),
                                           v[:, :, :, 0, side, :].bitcast(F32), ALU.subtract).then_inc(lo_cut, 1)

                def list_sums(b, j):
                    n = tile(b, j)
                    wait_n(pool, top_step, n * TOP_STEPS + 6)
                    pool.tensor_tensor(cand[:, :, :], best[:, 0, :].unsqueeze(2).broadcast_to([128, TOPK, TOPK]),
                                       best[:, 1, :].unsqueeze(1).broadcast_to([128, TOPK, TOPK]), ALU.add).then_inc(cand_made, 1)

                def take_queries(b):
                    wait_n(pool, q_copied, b.n * 4 + 4)
                    own_step(pool, att_made, b.n * 4)
                    pool.tensor_copy(q2[:, :], q[:, b.parity, :]).then_inc(q2_copied, 1)

                def body(b):
                    for k in range(KCH):
                        if k == 4 and (b + -1).exists:
                            take_queries(b + -1)
                        for event in front_events(b, k, 2):
                            list_sums(*event)
                        for event in front_events(b, k, 9):
                            lower_parts(*event)

                block_times(pool, body)

            @blk.vector
            def _(dve):
                def side_bests(b, j, half):
                    n = tile(b, j)
                    base = n * TOP_STEPS
                    side = lambda p: sim[:, j % 2, p, :]
                    if half == 0:
                        own_step(dve, sim_copied, n + 1)
                        own_step(dve, cand_made, n)
                        dve.max(best[:, 0, 0:8], side(0)).then_inc(top_step, 1)
                        dve.max(best[:, 1, 0:8], side(1)).then_inc(top_step, 1)
                        own_step(dve, top_step, base + 1)
                        dve.match_replace(cut[:, 0, :], best[:, 0, 0:8], side(0), LOWEST).then_inc(top_step, 1)
                    else:
                        own_step(dve, top_step, base + 2)
                        dve.match_replace(cut[:, 1, :], best[:, 1, 0:8], side(1), LOWEST).then_inc(top_step, 1)
                        own_step(dve, top_step, base + 3)
                        dve.max(best[:, 0, 8:16], cut[:, 0, :]).then_inc(top_step, 1)
                        own_step(dve, top_step, base + 4)
                        dve.max(best[:, 1, 8:16], cut[:, 1, :]).then_inc(top_step, 1)
                        wait_n(dve, top_step, base + 6)
                        dve.scalar_tensor_tensor(out=size[:, j % 2:j % 2 + 1], in0=best[:, 1, TOPK - 1:TOPK], scalar=-1.0, in1=best[:, 1, 0:1],
                                                 op0=ALU.mult, op1=ALU.max).then_inc(top_step, 1)

                def top_sums(b, j, part):
                    n = tile(b, j)
                    base = n * TOP_STEPS
                    flat = cand[:, :, :].rearrange("p a b -> p (a b)")
                    if part == 0:
                        own_step(dve, cand_made, n + 1)
                        own_step(dve, exped_top, n)
                        dve.max(top[:, 0:8], flat).then_inc(top_step, 1)
                    if part == 1:
                        own_step(dve, top_step, base + 8)
                        dve.match_replace(cand_cut[:, :], top[:, 0:8], flat, LOWEST).then_inc(top_step, 1)
                    if part == 2:
                        own_step(dve, top_step, base + 9)
                        dve.max(top[:, 8:16], cand_cut[:, :]).then_inc(top_step, 1)

                def threshold(b, j, half):
                    n = tile(b, j)
                    base = n * 4
                    if half == 0:
                        wait_n(dve, top_step, n * TOP_STEPS + 10)
                        dve.scalar_tensor_tensor(out=thr[:, 0:1], in0=top[:, 0:1], scalar=-88.0, in1=top[:, 15:16], op0=ALU.add, op1=ALU.max).then_inc(thr_step, 1)
                        wait_n(dve, thr_step, base + 1)
                        dve.tensor_scalar(thr[:, 1:2], thr[:, 0:1], 1.0 + 2.0 ** -22, None, ALU.mult).then_inc(thr_step, 1)
                        return
                    wait_n(dve, thr_step, base + 2)
                    dve.scalar_tensor_tensor(out=thr[:, 2:3], in0=thr[:, 0:1], scalar=1.0 - 3 * 2.0 ** -24, in1=thr[:, 1:2], op0=ALU.mult, op1=ALU.min).then_inc(thr_step, 1)
                    wait_n(dve, thr_step, base + 3)
                    dve.scalar_tensor_tensor(out=thr[:, 3:4], in0=size[:, j % 2:j % 2 + 1], scalar=-2.0 ** -24, in1=thr[:, 2:3], op0=ALU.mult, op1=ALU.add).then_inc(thr_step, 1)
                    wait_n(dve, thr_step, base + 4)
                    dve.tensor_scalar(nthr[:, :], thr[:, 3:4], -1.0, -8.0, ALU.mult, ALU.add).then_inc(topped, 1)
                    dve.tensor_scalar(sim[:, j % 2, 0, :], sim[:, j % 2, 0, :], thr[:, 3:4], None, ALU.subtract).then_inc(shifted, 1)

                def weights(b, c):
                    n = b.n * KCH + c
                    wait_n(dve, exped, n + 1)
                    wait_n(dve, kv_made, n - 3)
                    dve.scalar_tensor_tensor(out=w[:, c % 4, :], in0=sump[c % 3][:, :], scalar=0.0, in1=e[:, c % 4, :],
                                             op0=ALU.is_ge, op1=ALU.mult).then_inc(masked, 1)

                def invert(b):
                    wait_n(dve, exped_top, b.n * 4 + 4)
                    wait_n(dve, kv_scaled, b.n * 4)
                    dve.reciprocal(inv[:, :], total[:, b.parity, :]).then_inc(inverted, 1)

                def mask_att(b, j):
                    n, s = tile(b, j), j % 2
                    wait_n(dve, att_made, n + 1)
                    dve.tensor_tensor(att[:, s, :], tailp[s][:, 0:128], causal[:, :], ALU.add).then_inc(att_masked, 1)
                    wait_n(dve, att_masked, n + 1)
                    dve.tensor_reduce(amax[:, s, 0:1], att[:, s, :], AX.X, ALU.max).then_inc(att_max, 1)
                    wait_n(dve, att_max, n + 1)
                    dve.tensor_scalar(amax[:, s, 1:2], amax[:, s, 0:1], -1.0, None, ALU.mult).then_inc(att_neg, 1)

                def scale_att(b, j):
                    n, s = tile(b, j), j % 2
                    wait_n(dve, att_exp, n + 1)
                    dve.reciprocal(rowsum[:, s, 1:2], rowsum[:, s, 0:1]).then_inc(att_inv, 1)
                    wait_n(dve, att_inv, n + 1)
                    dve.tensor_scalar(probn[:, s, :], prob[:, s, :], rowsum[:, s, 1:2], None, ALU.mult).then_inc(att_scaled, 1)

                def add_out(b, j):
                    wait_n(dve, o_made, tile(b, j) + 1)
                    row = out[:, bass.ds(b.number * 4 + j, 1), :].rearrange("p o w -> p (o w)")
                    dve.tensor_tensor(row, tailp[j % 2][:, 0:W], row, ALU.add).then_inc(o_added, 1)

                def body(b):
                    for k in range(KCH):
                        if b.exists:
                            weights(b, k)
                        if k == 4 and (b + -1).exists:
                            invert(b + -1)
                        for step, act_on, part in ((0, side_bests, 0), (1, side_bests, 1), (3, top_sums, 0), (4, top_sums, 1),
                                                   (5, top_sums, 2), (6, threshold, 0), (8, threshold, 1)):
                            for event in front_events(b, k, step):
                                act_on(*event, part)
                        for step, act_on in ((5, mask_att), (7, scale_att), (13, add_out)):
                            for event in tail_events(b, k, step):
                                act_on(*event)

                wait_n(dve, consts_in, 64)
                dve.tensor_copy(pick[:, :, :].rearrange("p a b -> p (a b)"), pick_in[:, :]).then_inc(picked, 1)
                block_times(dve, body)

            @blk.scalar
            def _(act):
                copy = lambda dst, src: act.activation(dst, src, ACT.Copy)

                def copy_sim(b, j):
                    n = tile(b, j)
                    wait_n(act, sim_made, n + 1)
                    wait_n(act, lo_cut, (n - 1) * 2)
                    copy(sim[:, j % 2, :, :].rearrange("p a k -> p (a k)"), simp[:, 0:128]).then_inc(sim_copied, 1)

                def copy_q(b, j):
                    wait_n(act, sim_made, tile(b, j) + 1)
                    wait_n(act, q2_copied, b.n - 1)
                    act.activation(q[:, b.parity, cols(j)], simp[0:DIM, 128:256], ACT.Copy, scale=DIM ** -0.5).then_inc(q_copied, 1)

                def exp_top(b, j):
                    n = tile(b, j)
                    wait_n(act, topped, n + 1)
                    wait_n(act, inverted, b.n - 1)
                    wait_n(act, exped_top, n)
                    act.activation(topexp[:, :], top[:, :], ACT.Exp, bias=nthr[:, :],
                                   accum_out=total[:, b.parity, j:j + 1]).then_inc(exped_top, 1)

                def upper_parts(b, j):
                    n = tile(b, j)
                    wait_n(act, shifted, n + 1)
                    wait_n(act, z_turned, n)
                    for side in range(2):
                        copy(z[:, :, :, :, :, :][:, :, :, 0, side, :], halves[side](sim[:, j % 2, :, :])).then_inc(hi_cut, 1)

                def copy_zt(b, j):
                    n = tile(b, j)
                    wait_n(act, z_turned, n + 1)
                    wait_n(act, summed, (b.n - 1) * KCH)
                    copy(zt[:, b.parity, :, cols(j)], zbank[:, :].rearrange("p (c n) -> p c n", c=4)).then_inc(zt_copied, 1)

                def exp_sums(b, c):
                    n = b.n * KCH + c
                    wait_n(act, summed, n + 1)
                    wait_n(act, masked, n - 3)
                    act.activation(e[:, c % 4, :], sump[c % 3][:, :], ACT.Exp, bias=minus8[:, 0:1]).then_inc(exped, 1)

                def copy_kvt(b):
                    wait_n(act, kv_made, b.n * KCH + KCH)
                    wait_n(act, kv_turned, b.n * 4)
                    copy(kvt[:, :], kvp[:, :]).then_inc(kvt_copied, 1)

                def scale_kv(b, j):
                    wait_n(act, inverted, b.n + 1)
                    wait_n(act, kv_turned, tile(b, j) + 1)
                    act.activation(kv[:, j % 2, :], tailp[j % 2][:, 0:128], ACT.Copy, scale=inv[:, j:j + 1]).then_inc(kv_scaled, 1)

                def copy_ot(b, j):
                    wait_n(act, ot_made, tile(b, j) + 1)
                    copy(ot[:, j % 2, :], tailp[j % 2][0:DIM, 0:128]).then_inc(ot_copied, 1)

                def copy_kt(b, j):
                    wait_n(act, kt_made, tile(b, j) + 1)
                    copy(kt[:, j % 2, :], tailp[j % 2][0:DIM, 0:128]).then_inc(kt_copied, 1)

                def exp_att(b, j):
                    s = j % 2
                    wait_n(act, att_neg, tile(b, j) + 1)
                    act.activation(prob[:, s, :], att[:, s, :], ACT.Exp, bias=amax[:, s, 1:2], accum_out=rowsum[:, s, 0:1]).then_inc(att_exp, 1)

                def copy_probt(b, j):
                    wait_n(act, probt_made, tile(b, j) + 1)
                    copy(probt[:, j % 2, :], tailp[j % 2][:, 0:128]).then_inc(probt_copied, 1)

                def body(b):
                    for k in range(KCH):
                        if k == LAG and (b + -1).exists:
                            copy_kvt(b + -1)
                        if b.exists:
                            exp_sums(b, k)
                        for step, act_on in ((0, copy_sim), (3, copy_q), (9, upper_parts), (9, exp_top), (11, copy_zt)):
                            for event in front_events(b, k, step):
                                act_on(*event)
                        for step, act_on in ((0, scale_kv), (3, copy_kt), (6, exp_att), (9, copy_probt), (11, copy_ot)):
                            for event in tail_events(b, k, step):
                                act_on(*event)

                wait_n(act, filled, 1)
                block_times(act, body)

            @blk.tensor
            def _(pe):
                def sims(b, j):
                    n = tile(b, j)
                    if j == 0:
                        wait_n(pe, x_in[b.parity], b.uses * 16)
                        if b.opens_head:
                            wait_n(pe, head_in[b.u], (b.pair + 1) * (16 * HEAD_LOADS))
                    wait_n(pe, q_copied, n)
                    xj = x[:, b.parity, cols(j)]
                    pe.matmul(simp[:, 0:128], xj, both[:, b.u, :], start=True, stop=True)
                    pe.matmul(simp[0:DIM, 128:256], wq[:, b.u, :], xj, start=True, stop=True).then_inc(sim_made, 1)

                def turn_parts(b, j):
                    n = tile(b, j)
                    wait_n(pe, lo_cut, n * 2 + 2)
                    wait_n(pe, zt_copied, n)
                    flat = z[:, :, :, :, :, :].rearrange("p g h a s k -> p (g h a s k)").bitcast(F32)
                    for c in range(4):
                        mm = pe.transpose(zbank[:, cols(c)], flat[:, cols(c)], ident[:, :])
                    mm.then_inc(z_turned, 1)

                def sums(b, c):
                    n = b.n * KCH + c
                    if c == 0:
                        wait_n(pe, zt_copied, b.n * 4 + 4)
                    last = n - 3 if c >= 3 else n - c - KCH + (30, 31, 29)[c]
                    wait_n(pe, masked, last + 1)
                    halves_at = 2 * (c // 16) + c % 16 // 8
                    pe.matmul(sump[c % 3][:, :], pick[:, c % 8, :], zt[:, b.parity, halves_at, :], start=True, stop=True).then_inc(summed, 1)

                def lookup(b, c):
                    n = b.n * KCH + c
                    if c == 0:
                        wait_n(pe, kvt_copied, b.n)
                    wait_n(pe, masked, n + 1)
                    pe.matmul(kvp[:, :], table[:, b.u, c, :], w[:, c % 4, :], start=(c == 0), stop=(c == KCH - 1)).then_inc(kv_made, 1)

                def turn_kv(b, j):
                    wait_n(pe, kvt_copied, b.n + 1)
                    wait_n(pe, o_added, tile(b, j) - 1)
                    pe.transpose(tailp[j % 2][:, 0:128], kvt[:, cols(j)], ident[:, :]).then_inc(kv_turned, 1)

                def turn_keys(b, j):
                    wait_n(pe, kv_scaled, tile(b, j) + 1)
                    pe.transpose(tailp[j % 2][:, 0:128], kv[:, j % 2, :], ident[:, :]).then_inc(kt_made, 1)

                def att_scores(b, j):
                    wait_n(pe, kt_copied, tile(b, j) + 1)
                    wait_n(pe, q2_copied, b.n + 1)
                    pe.matmul(tailp[j % 2][:, 0:128], q2[:, cols(j)], kt[:, j % 2, :], start=True, stop=True).then_inc(att_made, 1)

                def turn_prob(b, j):
                    wait_n(pe, att_scaled, tile(b, j) + 1)
                    pe.transpose(tailp[j % 2][:, 0:128], probn[:, j % 2, :], ident[:, :]).then_inc(probt_made, 1)

                def att_values(b, j):
                    wait_n(pe, probt_copied, tile(b, j) + 1)
                    pe.matmul(tailp[j % 2][0:DIM, 0:128], kv[:, j % 2, DIM:2 * DIM], probt[:, j % 2, :], start=True, stop=True).then_inc(ot_made, 1)

                def project(b, j):
                    wait_n(pe, ot_copied, tile(b, j) + 1)
                    pe.matmul(tailp[j % 2][:, 0:W], ot[:, j % 2, :], wo[:, b.u, :], start=True, stop=True).then_inc(o_made, 1)

                def body(b):
                    for k in range(KCH):
                        if b.exists:
                            sums(b, k)
                        if k >= LAG and b.exists:
                            lookup(b, k - LAG)
                        elif k < LAG and (b + -1).exists:
                            lookup(b + -1, KCH + k - LAG)
                        for step, act_on in ((0, sims), (11, turn_parts)):
                            for event in front_events(b, k, step):
                                act_on(*event)
                        for step, act_on in ((0, turn_kv), (3, turn_keys), (5, att_scores), (9, turn_prob), (11, att_values), (13, project)):
                            for event in tail_events(b, k, step):
                                act_on(*event)

                wait_n(pe, consts_in, 64)
                wait_n(pe, picked, 1)
                block_times(pe, body)


def ffn_views(nc, T):
    both = nc.dram_tensor("both", [DIM, HEADS, 128], F32, kind="Internal").ap()
    xt = nc.dram_tensor("xt", [W, TT, 128], F32, kind="Internal").ap()
    tiles = lambda v: v.rearrange("(t i) h w -> (i h) t w", i=2)
    T["both"], T["both_heads"] = both, both.rearrange("d h k -> h d k")
    T["xt"], T["xt_blocks"] = xt, xt.rearrange("w (b t) n -> b w (t n)", t=4)
    T["att_tiles"], T["out_tiles"] = tiles(T["att_rows"]), tiles(T["out_rows"])
    chunks = lambda v: v.rearrange("(h c b g a) d -> h b g a c d", h=HEADS, b=4, g=2, a=32)
    T["keys_chunks"], T["values_chunks"] = chunks(T["keys_table"]), chunks(T["values_table"])
    T["Wq_heads"] = T["Wq"].rearrange("d (h e) -> h d e", h=HEADS)
    T["Wo_heads"] = T["Wo"].rearrange("(h d) e -> h d e", h=HEADS)


def build(nc, args, out):
    T = dict(args)
    dram = lambda name, shape: nc.dram_tensor(name, shape, F32, kind="Internal").ap()
    T["h"] = [dram("h_even", [QUADS, 128, PX]), dram("h_odd", [QUADS, 128, PX])]
    for name, t in (("X", dram("spectrum_in", [M2, ROWS, IMAGES, C])), ("Y", dram("spectrum_out", [M2, ROWS, IMAGES, C]))):
        T[name] = t.rearrange("k r (q i) c -> q r k (i c)", i=QI)
        T[name + "k"] = t.rearrange("k r n c -> k n r c")
    T["x"] = T["x"].rearrange("(q i) (j r) w c -> q (i j) (r w c)", i=QI, r=2)
    T["tok_rows"] = dram("tok", [IMAGES, H, W])
    T["tok"] = T["tok_rows"].rearrange("(q i) h w -> q i (h w)", i=QI)
    T["att_rows"] = dram("att", [IMAGES, H, W])
    T["out_rows"] = out
    ffn_views(nc, T)
    tower_pass(nc, -1, T)
    for layer in range(LAYERS):
        mix_pass(nc, layer, T)
        tower_pass(nc, layer, T)
    attention_pass(nc, T)
    ffn_prepare(nc, T)
    ffn_pass(nc, T)


_TOK = ["fc0_w", "fc0_b", "ln0_g", "ln0_b", "w1r", "w1i", "w2r", "w2i", "conv_w", "conv_b", "ln_g", "ln_b",
        "fc1_w", "fc1_b", "fc2_w", "fc2_b", "fc3_w", "fc3_b"]
_FFN = ["Wq_pk", "pk_keys", "Wq", "keys_table", "values_table", "Wo"]


def kernel(**inputs):
    import concourse.bacc as bacc
    from concourse.bass_utils import run_bass_kernel_spmd

    nc = bacc.Bacc("TRN2", target_bir_lowering=False, num_devices=1)
    named = {"x": inputs["x"]}
    named.update({n: inputs["L0_tok_" + n] for n in _TOK})
    named.update({n: inputs["L0_ffn_" + n] for n in _FFN})
    named.update(shape_constants())
    arrays, args = {}, {}
    for name, a in named.items():
        a = np.ascontiguousarray(a)
        arrays[name + "_dram"] = a
        args[name] = nc.dram_tensor(name + "_dram", a.shape, mybir.dt.from_np(a.dtype), kind="ExternalInput").ap()
    out = nc.dram_tensor("out_dram", (IMAGES, H, W), F32, kind="ExternalOutput").ap()
    build(nc, args, out)
    r = run_bass_kernel_spmd(nc, [arrays], core_ids=[0])
    return r.results[0]["out_dram"]
```
